# Optimizing a Trainium2 kernel written in Bass

```python
import numpy as np
import jax
import jax.numpy as jnp

def _softmax(x, axis=-1):
    return jax.nn.softmax(x, axis=axis)

def _gelu(x):
    return jax.nn.gelu(x, approximate=True)

def _silu(x):
    return jax.nn.silu(x)

def _sigmoid(x):
    return jax.nn.sigmoid(x)

def _layernorm(x, axis=-1, eps=1e-05):
    m = jnp.mean(x, axis=axis, keepdims=True)
    v = jnp.var(x, axis=axis, keepdims=True)
    return (x - m) / jnp.sqrt(v + eps)

def _scatter_add(tgt, idx, src, axis=0):
    return tgt.at[idx].add(src)

def _segment_sum(src, seg, n):
    return jax.ops.segment_sum(src, seg, n)
kernel_name = 'mk_vit_tower_cls_d2_tok_img256_r4_fa7752'

def setup_inputs(seed: int=0):
    np.random.seed(seed)
    _w = jnp.asarray

    def _rec_inputs():
        import jax
        import jax.numpy as jnp
        _rk = jax.random.key(seed)
        x = -0.000209053 + 0.999977 * jax.random.normal(jax.random.fold_in(_rk, 1), (16, 64, 56, 56), jnp.float32)
        cls_tok = 0.02 * jax.random.normal(jax.random.fold_in(_rk, 5), (1, 1, 64), jnp.float32)
        return (x, cls_tok)
    x, cls_tok = _rec_inputs()

    def _L0_tok_setup():
        import jax, jax.numpy as jnp
        import numpy as np
        B, EMB, HT, WD = (32, 64, 56, 56)
        NH, WS, SHIFTED = (8, 4, True)

        def _rel_indices(ws):
            coords = np.array([[i, j] for i in range(ws) for j in range(ws)])
            rel = coords[None, :, :] - coords[:, None, :] + ws - 1
            return jnp.asarray(rel)

        def _shift_masks(ws):
            m = np.zeros((ws * ws, ws * ws), np.float32)
            s = ws * (ws // 2)
            m[-s:, :-s] = -np.inf
            m[:-s, -s:] = -np.inf
            col = m.reshape(ws, ws, ws, ws).transpose(1, 0, 3, 2).reshape(ws * ws, ws * ws)
            return (jnp.asarray(m), jnp.asarray(col))
        key = jax.random.key(seed)
        ks = jax.random.split(key, 6)
        x = jax.random.normal(ks[0], (B, EMB, HT, WD), jnp.float32)
        s = 1.0 / np.sqrt(EMB)
        w1 = jax.random.uniform(ks[1], (3 * EMB, EMB), jnp.float32, -s, s)
        b1 = jax.random.uniform(ks[2], (3 * EMB,), jnp.float32, -s, s)
        w2 = jax.random.uniform(ks[3], (EMB, EMB), jnp.float32, -s, s)
        b2 = jax.random.uniform(ks[4], (EMB,), jnp.float32, -s, s)
        pos_emb = jax.random.normal(ks[5], (2 * WS - 1, 2 * WS - 1), jnp.float32)
        return {'x': x, 'w1': w1, 'b1': b1, 'w2': w2, 'b2': b2, 'pos_emb': pos_emb}
    _L0_tok_all = _L0_tok_setup()
    _L0_tok_in = {k: v for k, v in _L0_tok_all.items() if k in ('w1', 'b1', 'w2', 'b2', 'pos_emb')}
    del _L0_tok_all

    def _L0_attn_setup():
        import jax, jax.numpy as jnp
        import numpy as np

        def softcap(x, a=10.0):
            return a * jnp.tanh(x / a)
        key = jax.random.key(seed)
        B, T, D = (4, 512, 64)
        ks = jax.random.split(key, 5)
        w = lambda k, s: jax.random.normal(k, s, dtype=jnp.float32) * 0.02
        return {'x': jax.random.normal(ks[0], (B, T, D), dtype=jnp.float32), 'Wq': w(ks[1], (D, D)), 'bq': jnp.zeros((D,), jnp.float32), 'Wk': w(ks[2], (D, D)), 'bk': jnp.zeros((D,), jnp.float32), 'Wv': w(ks[3], (D, D)), 'bv': jnp.zeros((D,), jnp.float32), 'Wg': w(ks[4], (D, 3 * D)), 'bg': jnp.zeros((3 * D,), jnp.float32), 'input_bias': -jnp.ones((D,), jnp.float32), 'norm_scale': jnp.ones((D,), jnp.float32)}
    _L0_attn_all = _L0_attn_setup()
    _L0_attn_in = {k: v for k, v in _L0_attn_all.items() if k in ('Wq', 'bq', 'Wk', 'bk', 'Wv', 'bv', 'Wg', 'bg', 'input_bias', 'norm_scale')}
    del _L0_attn_all

    def _L0_ffn_setup():
        import math
        import jax, jax.numpy as jnp
        import numpy as np
        CAPACITY_FACTOR = 1.25
        key = jax.random.key(seed)
        ks = jax.random.split(key, 5)
        B, L, D, F, E = (8, 2048, 64, 256, 8)
        h = jax.random.normal(ks[0], (B, L, D), dtype=jnp.float32)
        gate_w = jax.random.normal(ks[1], (D, E), dtype=jnp.float32) * 0.02
        gate_b = jnp.zeros((E,), dtype=jnp.float32)
        w1 = jax.random.normal(ks[2], (E, D, F), dtype=jnp.float32) * (1.0 / math.sqrt(D))
        b1 = jnp.zeros((E, F), dtype=jnp.float32)
        w2 = jax.random.normal(ks[3], (E, F, D), dtype=jnp.float32) * (1.0 / math.sqrt(F))
        b2 = jnp.zeros((E, D), dtype=jnp.float32)
        return {'h': h, 'gate_w': gate_w, 'gate_b': gate_b, 'w1': w1, 'b1': b1, 'w2': w2, 'b2': b2}
    _L0_ffn_all = _L0_ffn_setup()
    _L0_ffn_in = {k: v for k, v in _L0_ffn_all.items() if k in ('gate_w', 'gate_b', 'w1', 'b1', 'w2', 'b2')}
    del _L0_ffn_all

    def _L1_attn_setup():
        import jax, jax.numpy as jnp
        import numpy as np
        SEQ, BATCH, IN, HID = (512, 64, 64, 64)
        key = jax.random.key(seed)
        k1, k2, k3, k4, k5 = jax.random.split(key, 5)
        s = 1.0 / np.sqrt(HID)
        return {'x_in': jax.random.normal(k1, (SEQ, BATCH, IN), dtype=jnp.float32), 'W_ih': jax.random.uniform(k2, (HID, IN), jnp.float32, -s, s), 'W_hh': jax.random.uniform(k3, (HID, HID), jnp.float32, -s, s), 'b_ih': jax.random.uniform(k4, (HID,), jnp.float32, -s, s), 'b_hh': jax.random.uniform(k5, (HID,), jnp.float32, -s, s)}
    _L1_attn_all = _L1_attn_setup()
    _L1_attn_in = {k: v for k, v in _L1_attn_all.items() if k in ('W_ih', 'W_hh', 'b_ih', 'b_hh')}
    del _L1_attn_all

    def _L1_ffn_setup():
        import jax, jax.numpy as jnp
        import numpy as np
        DIM = 64
        H = 8
        D = 64
        G = 64
        INNER = H * D
        SCALE = D ** (-0.5)
        key = jax.random.key(seed)
        ks = jax.random.split(key, 12)
        B, N = (4, 4096)
        x = jax.random.normal(ks[0], (B, N, DIM), dtype=jnp.float32)
        s = lambda fan_in: 1.0 / np.sqrt(fan_in)
        W_fx = jax.random.normal(ks[1], (DIM, INNER), dtype=jnp.float32) * s(DIM)
        b_fx = jnp.zeros((INNER,), dtype=jnp.float32)
        W_x = jax.random.normal(ks[2], (DIM, INNER), dtype=jnp.float32) * s(DIM)
        b_x = jnp.zeros((INNER,), dtype=jnp.float32)
        A = jax.random.normal(ks[3], (G, D), dtype=jnp.float32)
        Q, _ = jnp.linalg.qr(A.T)
        W_slice = Q[:, :G].astype(jnp.float32)
        b_slice = jnp.zeros((G,), dtype=jnp.float32)
        W_q = jax.random.normal(ks[4], (D, D), dtype=jnp.float32) * s(D)
        W_k = jax.random.normal(ks[5], (D, D), dtype=jnp.float32) * s(D)
        W_v = jax.random.normal(ks[6], (D, D), dtype=jnp.float32) * s(D)
        W_out = jax.random.normal(ks[7], (INNER, DIM), dtype=jnp.float32) * s(INNER)
        b_out = jnp.zeros((DIM,), dtype=jnp.float32)
        temperature = jnp.ones((1, H, 1, 1), dtype=jnp.float32) * 0.5
        return {'x': x, 'W_fx': W_fx, 'b_fx': b_fx, 'W_x': W_x, 'b_x': b_x, 'W_slice': W_slice, 'b_slice': b_slice, 'W_q': W_q, 'W_k': W_k, 'W_v': W_v, 'W_out': W_out, 'b_out': b_out, 'temperature': temperature}
    _L1_ffn_all = _L1_ffn_setup()
    _L1_ffn_in = {k: v for k, v in _L1_ffn_all.items() if k in ('W_fx', 'b_fx', 'W_x', 'b_x', 'W_slice', 'b_slice', 'W_q', 'W_k', 'W_v', 'W_out', 'b_out', 'temperature')}
    del _L1_ffn_all
    return {'x': x, 'cls_tok': cls_tok, 'L0_tok_w1': _L0_tok_in['w1'], 'L0_tok_b1': _L0_tok_in['b1'], 'L0_tok_w2': _L0_tok_in['w2'], 'L0_tok_b2': _L0_tok_in['b2'], 'L0_tok_pos_emb': _L0_tok_in['pos_emb'], 'L0_attn_Wq': _L0_attn_in['Wq'], 'L0_attn_bq': _L0_attn_in['bq'], 'L0_attn_Wk': _L0_attn_in['Wk'], 'L0_attn_bk': _L0_attn_in['bk'], 'L0_attn_Wv': _L0_attn_in['Wv'], 'L0_attn_bv': _L0_attn_in['bv'], 'L0_attn_Wg': _L0_attn_in['Wg'], 'L0_attn_bg': _L0_attn_in['bg'], 'L0_attn_input_bias': _L0_attn_in['input_bias'], 'L0_attn_norm_scale': _L0_attn_in['norm_scale'], 'L0_ffn_gate_w': _L0_ffn_in['gate_w'], 'L0_ffn_gate_b': _L0_ffn_in['gate_b'], 'L0_ffn_w1': _L0_ffn_in['w1'], 'L0_ffn_b1': _L0_ffn_in['b1'], 'L0_ffn_w2': _L0_ffn_in['w2'], 'L0_ffn_b2': _L0_ffn_in['b2'], 'L1_attn_W_ih': _L1_attn_in['W_ih'], 'L1_attn_W_hh': _L1_attn_in['W_hh'], 'L1_attn_b_ih': _L1_attn_in['b_ih'], 'L1_attn_b_hh': _L1_attn_in['b_hh'], 'L1_ffn_W_fx': _L1_ffn_in['W_fx'], 'L1_ffn_b_fx': _L1_ffn_in['b_fx'], 'L1_ffn_W_x': _L1_ffn_in['W_x'], 'L1_ffn_b_x': _L1_ffn_in['b_x'], 'L1_ffn_W_slice': _L1_ffn_in['W_slice'], 'L1_ffn_b_slice': _L1_ffn_in['b_slice'], 'L1_ffn_W_q': _L1_ffn_in['W_q'], 'L1_ffn_W_k': _L1_ffn_in['W_k'], 'L1_ffn_W_v': _L1_ffn_in['W_v'], 'L1_ffn_W_out': _L1_ffn_in['W_out'], 'L1_ffn_b_out': _L1_ffn_in['b_out'], 'L1_ffn_temperature': _L1_ffn_in['temperature']}

def reference(x, cls_tok, L0_tok_w1, L0_tok_b1, L0_tok_w2, L0_tok_b2, L0_tok_pos_emb, L0_attn_Wq, L0_attn_bq, L0_attn_Wk, L0_attn_bk, L0_attn_Wv, L0_attn_bv, L0_attn_Wg, L0_attn_bg, L0_attn_input_bias, L0_attn_norm_scale, L0_ffn_gate_w, L0_ffn_gate_b, L0_ffn_w1, L0_ffn_b1, L0_ffn_w2, L0_ffn_b2, L1_attn_W_ih, L1_attn_W_hh, L1_attn_b_ih, L1_attn_b_hh, L1_ffn_W_fx, L1_ffn_b_fx, L1_ffn_W_x, L1_ffn_b_x, L1_ffn_W_slice, L1_ffn_b_slice, L1_ffn_W_q, L1_ffn_W_k, L1_ffn_W_v, L1_ffn_W_out, L1_ffn_b_out, L1_ffn_temperature):
    import jax
    import jax.numpy as jnp

    def _L0_tok_ref(x, w1, b1, w2, b2, pos_emb):
        import jax, jax.numpy as jnp
        import numpy as np
        B, EMB, HT, WD = (32, 64, 56, 56)
        NH, WS, SHIFTED = (8, 4, True)

        def _rel_indices(ws):
            coords = np.array([[i, j] for i in range(ws) for j in range(ws)])
            rel = coords[None, :, :] - coords[:, None, :] + ws - 1
            return jnp.asarray(rel)

        def _shift_masks(ws):
            m = np.zeros((ws * ws, ws * ws), np.float32)
            s = ws * (ws // 2)
            m[-s:, :-s] = -np.inf
            m[:-s, -s:] = -np.inf
            col = m.reshape(ws, ws, ws, ws).transpose(1, 0, 3, 2).reshape(ws * ws, ws * ws)
            return (jnp.asarray(m), jnp.asarray(col))
        b, c, ht, wd = x.shape
        ws, nh = (WS, NH)
        e = c // nh
        xt = x.reshape(b, c, ht * wd).transpose(0, 2, 1)
        qkv = xt @ w1.T + b1
        qkv = qkv.reshape(b, ht, wd, c, 3)
        if SHIFTED:
            qkv = jnp.roll(qkv, (-ws // 2, -ws // 2), axis=(1, 2))
        Wh, Ww = (ht // ws, wd // ws)
        qkv = qkv.reshape(b, Wh, ws, Ww, ws, e, nh, 3)
        qkv = qkv.transpose(0, 6, 1, 3, 2, 4, 5, 7).reshape(b, nh, Wh, Ww, ws * ws, e, 3)
        Q, K, V = (qkv[..., 0], qkv[..., 1], qkv[..., 2])
        scale = jnp.sqrt(jnp.float32(c / nh))
        wei = jnp.einsum('bhijpe,bhijqe->bhijpq', Q, K) / scale
        rel = _rel_indices(ws)
        wei = wei + pos_emb[rel[..., 0], rel[..., 1]]
        if SHIFTED:
            row_mask, col_mask = _shift_masks(ws)
            wei = wei.at[:, :, -1, :].add(row_mask)
            wei = wei.at[:, :, :, -1].add(col_mask)
        attn = jax.nn.softmax(wei, axis=-1)
        out = jnp.einsum('bhijpq,bhijqe->bhijpe', attn, V)
        out = out.reshape(b, nh, Wh, Ww, ws, ws, e)
        out = out.transpose(0, 2, 4, 3, 5, 1, 6).reshape(b, ht, wd, nh * e)
        out = out.reshape(b, ht * wd, c)
        return out @ w2.T + b2

    def _L0_attn_ref(x, Wq, bq, Wk, bk, Wv, bv, Wg, bg, input_bias, norm_scale):
        import jax, jax.numpy as jnp
        import numpy as np

        def softcap(x, a=10.0):
            return a * jnp.tanh(x / a)
        B, T, D = x.shape
        inv_sqrt_d = 1.0 / jnp.sqrt(jnp.asarray(D, jnp.float32))
        q = x @ Wq + bq
        k = (x @ Wk + bk) * inv_sqrt_d
        v = x @ Wv + bv
        gates = x @ Wg + bg
        i_pre, f_pre, o_pre = jnp.split(gates, 3, axis=-1)
        log_i = softcap(i_pre + input_bias)
        log_f = -jax.nn.softplus(f_pre)

        def step(carry, inp):
            M, n, m = carry
            qt, kt, vt, li, lf, op = inp
            m_next = jnp.maximum(lf + m, li)
            i_s = jnp.exp(li - m_next)
            f_s = jnp.exp(lf + m - m_next)
            M = f_s[:, :, None] * M + i_s[:, :, None] * (vt[:, :, None] * kt[:, None, :])
            n = f_s * n + i_s * kt
            h_raw = jnp.einsum('bij,bj->bi', M, qt)
            denom = jnp.maximum(jnp.abs(jnp.einsum('bi,bi->b', n, qt))[:, None], 1e-06)
            h = jax.nn.sigmoid(op) * (h_raw / denom)
            return ((M, n, m_next), h)
        M0 = jnp.zeros((B, D, D), jnp.float32)
        n0 = jnp.zeros((B, D), jnp.float32)
        m0 = jnp.zeros((B, D), jnp.float32)
        xs = tuple((jnp.swapaxes(a, 0, 1) for a in (q, k, v, log_i, log_f, o_pre)))
        _, hs = jax.lax.scan(step, (M0, n0, m0), xs)
        out = jnp.swapaxes(hs, 0, 1)
        rms = jnp.sqrt(jnp.mean(out * out, axis=-1, keepdims=True) + 1e-08)
        return out / rms * norm_scale

    def _L0_ffn_ref(h, gate_w, gate_b, w1, b1, w2, b2):
        import math
        import jax, jax.numpy as jnp
        import numpy as np
        CAPACITY_FACTOR = 1.25
        B, L, D = h.shape
        E = gate_w.shape[1]
        T = B * L
        C = max(1, math.ceil(CAPACITY_FACTOR * T / E))
        x = h.reshape(T, D)
        logits = x @ gate_w + gate_b
        probs = jax.nn.softmax(logits, axis=-1)
        idx = jnp.argmax(probs, axis=-1)
        prb = jnp.take_along_axis(probs, idx[:, None], axis=1)[:, 0]
        one_hot = jax.nn.one_hot(idx, E, dtype=jnp.float32)
        pos = (jnp.cumsum(one_hot, axis=0) * one_hot).sum(-1).astype(jnp.int32) - 1
        kept = pos < C
        pos_safe = jnp.where(kept, pos, C)
        buf = jnp.zeros((E, C, D), dtype=h.dtype).at[idx, pos_safe].set(x, mode='drop')
        hmid = jax.nn.relu(jnp.einsum('ecd,edf->ecf', buf, w1) + b1[:, None, :])
        ybuf = jnp.einsum('ecf,efd->ecd', hmid, w2) + b2[:, None, :]
        pos_g = jnp.minimum(pos, C - 1)
        y_tok = ybuf[idx, pos_g] * (prb * kept)[:, None]
        y = y_tok.reshape(B, L, D)
        y = jnp.nan_to_num(y, nan=0.0, posinf=10000.0, neginf=-10000.0)
        return y

    def _L1_attn_ref(x_in, W_ih, W_hh, b_ih, b_hh):
        import jax, jax.numpy as jnp
        import numpy as np
        SEQ, BATCH, IN, HID = (512, 64, 64, 64)
        xp = jnp.einsum('tbi,hi->tbh', x_in, W_ih) + b_ih + b_hh
        h0 = jnp.zeros((x_in.shape[1], W_hh.shape[0]), dtype=x_in.dtype)

        def step(h, xp_t):
            h_new = jnp.tanh(xp_t + h @ W_hh.T)
            return (h_new, h_new)
        _, hiddens = jax.lax.scan(step, h0, xp)
        return hiddens

    def _L1_ffn_ref(x, W_fx, b_fx, W_x, b_x, W_slice, b_slice, W_q, W_k, W_v, W_out, b_out, temperature):
        import jax, jax.numpy as jnp
        import numpy as np
        DIM = 64
        H = 8
        D = 64
        G = 64
        INNER = H * D
        SCALE = D ** (-0.5)
        B, N, _ = x.shape
        fx_mid = (x @ W_fx + b_fx).reshape(B, N, H, D).transpose(0, 2, 1, 3)
        x_mid = (x @ W_x + b_x).reshape(B, N, H, D).transpose(0, 2, 1, 3)
        temp = jnp.clip(temperature, 0.1, 5.0)
        slice_weights = jax.nn.softmax((x_mid @ W_slice + b_slice) / temp, axis=-1)
        slice_norm = slice_weights.sum(axis=2)
        slice_token = jnp.einsum('bhnc,bhng->bhgc', fx_mid, slice_weights)
        slice_token = slice_token / (slice_norm[..., None] + 1e-05)
        q = slice_token @ W_q
        k = slice_token @ W_k
        v = slice_token @ W_v
        attn = jax.nn.softmax(jnp.einsum('bhgc,bhkc->bhgk', q, k) * SCALE, axis=-1)
        out_slice = jnp.einsum('bhgk,bhkc->bhgc', attn, v)
        out_x = jnp.einsum('bhgc,bhng->bhnc', out_slice, slice_weights)
        out_x = out_x.transpose(0, 2, 1, 3).reshape(B, N, INNER)
        return out_x @ W_out + b_out
    h = _L0_tok_ref(x, L0_tok_w1, L0_tok_b1, L0_tok_w2, L0_tok_b2, L0_tok_pos_emb)
    h = jnp.concatenate([jnp.broadcast_to(cls_tok, (h.shape[0], 1, h.shape[2])), h], axis=1)
    h = h + _L0_attn_ref(_layernorm(h, axis=-1), L0_attn_Wq, L0_attn_bq, L0_attn_Wk, L0_attn_bk, L0_attn_Wv, L0_attn_bv, L0_attn_Wg, L0_attn_bg, L0_attn_input_bias, L0_attn_norm_scale)
    h = h + _L0_ffn_ref(_layernorm(h, axis=-1), L0_ffn_gate_w, L0_ffn_gate_b, L0_ffn_w1, L0_ffn_b1, L0_ffn_w2, L0_ffn_b2)
    h = h + _L1_attn_ref(_layernorm(h, axis=-1), L1_attn_W_ih, L1_attn_W_hh, L1_attn_b_ih, L1_attn_b_hh)
    h = h + _L1_ffn_ref(_layernorm(h, axis=-1), L1_ffn_W_fx, L1_ffn_b_fx, L1_ffn_W_x, L1_ffn_b_x, L1_ffn_W_slice, L1_ffn_b_slice, L1_ffn_W_q, L1_ffn_W_k, L1_ffn_W_v, L1_ffn_W_out, L1_ffn_b_out, L1_ffn_temperature)
    return h

_drawn_inputs = setup_inputs


def setup_inputs(seed=0):
    import zlib

    import numpy as np

    out = dict(_drawn_inputs(seed))
    spreads = {'L0_attn_bq': (0.0, 0.1),
     'L0_attn_bk': (0.0, 0.1),
     'L0_attn_bv': (0.0, 0.1),
     'L0_attn_bg': (0.0, 0.1),
     'L0_attn_input_bias': (-1.0, 0.6),
     'L0_attn_norm_scale': (1.0, 0.2),
     'L0_ffn_gate_b': (0.0, 0.1),
     'L0_ffn_b1': (0.0, 0.8),
     'L0_ffn_b2': (0.0, 0.707),
     'L1_ffn_b_fx': (0.0, 0.1),
     'L1_ffn_b_x': (0.0, 0.8),
     'L1_ffn_b_slice': (0.0, 0.8),
     'L1_ffn_b_out': (0.0, 0.1),
     'L1_ffn_temperature': (0.5, 0.6)}
    factors = {}
    for name, (base, spread) in spreads.items():
        noise = np.random.default_rng([zlib.crc32(name.encode()), seed]).standard_normal(out[name].shape)
        drawn = base * np.exp(spread * noise) if base else spread * noise
        out[name] = jnp.asarray(drawn.astype(out[name].dtype))
    for name, factor in factors.items():
        out[name] = (out[name] * factor).astype(out[name].dtype)
    return out
```

```python
import concourse.bass as bass
from concourse import mybir
from contextlib import ExitStack

F32 = mybir.dt.float32
I32 = mybir.dt.int32
ALU = mybir.AluOpType
ACT = mybir.ActivationFunctionType
AX = mybir.AxisListType

B, D, SIDE = 16, 64, 56
PAIRS = B // 2
T = SIDE * SIDE + 1
TILE = 128
CHUNKS = -(-T // TILE)
TP = CHUNKS * TILE
TAIL = T - (CHUNKS - 1) * TILE
H, HE = 8, 8
WS = 4
NW = SIDE // WS
Q = WS * WS
GRP = NW * Q
E, F = 8, 256
CAP = -(-5 * B * T // (4 * E))
BLK = 512
CAPP = -(-CAP // BLK) * BLK
SH, G = 8, 64
EPS = 1e-5
NEG = -1e30
LN_EXP = "natural_log_exp_and_others"
TANH = "exp_and_others"


class Mem:

    def __init__(self, nc, ctx, stage):
        self.nc, self.ctx, self.stage, self.starts = nc, ctx, stage, []

    def sb(self, name, shape, dt=F32):
        return self.ctx.enter_context(self.nc.sbuf_tensor(f"{self.stage}_{name}", shape, dt))

    def ps(self, name, shape):
        return self.ctx.enter_context(self.nc.psum_tensor(f"{self.stage}_{name}", shape, F32))

    def sems(self, names, start=0):
        got = [self.ctx.enter_context(self.nc.semaphore(f"{self.stage}_{n}")) for n in names.split()]
        self.starts += [(s, start) for s in got]
        return got

    def open(self):
        with self.nc.Block() as block:

            @block.gpsimd
            def _(pool):
                for s, start in self.starts:
                    pool.sem_clear(s)
                    if start:
                        pool.sem_inc(s, start)


def new(i, k=1):
    return (i + 2) * k


def old(i, k=1):
    return (i + 1) * k


def stand(eng, passed):
    eng.sem_inc(passed, 1)


def bc(ap, shape):
    return ap.to_broadcast(shape)


def window_attention(nc, a, h0):
    with ExitStack() as ctx:
        m = Mem(nc, ctx, "A")
        wq, wk, wv, wo = (m.sb(n, [128, 128]) for n in ("wq", "wk", "wv", "wo"))
        bq, bk, bv, bo = (m.sb(n, [128, 1]) for n in ("bq", "bk", "bv", "bo"))
        bqs = m.sb("bqs", [128, 1])
        head_of_row = m.sb("head_of_row", [128, H])
        head_of_key = m.sb("head_of_key", [128, D])
        winmask = m.sb("winmask", [128, 2, NW, Q])
        pos = m.sb("pos", [128, Q])
        bias = m.sb("bias", [128, 2, NW, Q])
        xg = m.sb("xg", [128, NW, Q])
        xrep = m.sb("xrep", [128, NW, H, Q])
        qbd = m.sb("qbd", [128, NW, 2, Q])
        ksb = m.sb("ksb", [128, NW, Q])
        kmask = m.sb("kmask", [128, NW, H, Q])
        vbd = m.sb("vbd", [128, NW * 2, D])
        s1 = m.sb("s1", [128, NW, 2, Q])
        st = m.sb("st", [128, NW * 2, Q])
        mx = m.sb("mx", [128, NW * 2])
        sm = m.sb("sm", [128, NW * 2])
        rs = m.sb("rs", [128, NW * 2])
        pt = m.sb("pt", [128, NW, 2 * Q])
        osb = m.sb("osb", [128, NW, Q])
        res = m.sb("res", [128, WS, NW, WS])
        clst = m.sb("clst", [128, 1])
        zero = m.sb("zero", [128, TP - T])
        psqk = m.ps("psqk", [128, 512])
        pss = m.ps("pss", [128, 512])
        psv = m.ps("psv", [128, 2048])
        pso = m.ps("pso", [128, 512])
        psp = m.ps("psp", [128, 512])
        consts, edges, memz, ready, bias_ready = m.sems("consts edges memz ready bias_ready")
        x_in, stored = m.sems("x_in stored", 16)
        (qk_done, k_sb, xr_done, v_done, kmask_done, s_done, vbd_done, s1_done, st_done, mx_done, sub_done,
         exp_done, sum_done, rcp_done, nrm_done, pt_done, o_done, p_done, res_done) = m.sems(
            "qk_done k_sb xr_done v_done kmask_done s_done vbd_done s1_done st_done mx_done sub_done "
            "exp_done sum_done rcp_done nrm_done pt_done o_done p_done res_done", 1)
        q_sb, osb_done = m.sems("q_sb osb_done", 2)
        NCONST = 2 * 9 + 3 + WS * WS
        m.open()
        with nc.Block() as block:

            @block.sync
            def _(sp):
                sp.wait_ge(memz, 1)
                for b in range(2):
                    r = slice(64 * b, 64 * b + 64)
                    for t, w in enumerate((wq, wk, wv)):
                        sp.dma_start(w[r, r], a["w1"][t]).then_inc(consts, 16)
                    sp.dma_start(wo[r, r], a["w2"]).then_inc(consts, 16)
                    for t, w in enumerate((bq, bk, bv)):
                        sp.dma_start(w[r, :], a["b1"][t].unsqueeze(1)).then_inc(consts, 16)
                    sp.dma_start(bo[r, :], a["b2"].unsqueeze(1)).then_inc(consts, 16)
                    sp.dma_start(clst[r, :], a["cls"].unsqueeze(1)).then_inc(consts, 16)
                sp.dma_start(head_of_row[:], a["c_head_of_row"]).then_inc(consts, 16)
                sp.dma_start(head_of_key[:], a["c_head_of_key"]).then_inc(consts, 16)
                sp.dma_start(winmask[:], a["c_winmask"]).then_inc(consts, 16)
                for qi in range(WS):
                    for qj in range(WS):
                        sp.dma_start(pos[WS * qi + qj:128:Q, :],
                                     bc(a["posr"][3 - qi:7 - qi, 3 - qj:7 - qj].unsqueeze(0),
                                        [H, WS, WS])).then_inc(consts, 16)
                sp.wait_ge(consts, 16 * NCONST)
                for p in range(PAIRS):
                    with nc.allow_non_contiguous_dma(reason="one column"):
                        sp.dma_start(h0[p, :, 0:1], clst[:]).then_inc(edges, 16)
                    sp.dma_start(h0[p, :, T:TP], zero[:]).then_inc(edges, 16)
                with sp.Fori(0, PAIRS) as p:
                    with sp.Fori(0, NW) as g:
                        n = p * NW + g
                        sp.wait_ge(v_done, old(n))
                        sp.wait_ge(qk_done, old(n))
                        sp.dma_start(xg[:], a["xw"][p * NW + g]).then_inc(x_in, 16)
                sp.wait_ge(edges, 32 * PAIRS)

            @block.gpsimd
            def _(pool):
                with pool.Fori(0, PAIRS) as p:
                    with pool.Fori(0, NW) as g:
                        n = p * NW + g
                        pool.wait_ge(k_sb, new(n))
                        pool.wait_ge(s_done, old(n))
                        nc.gpsimd.tensor_tensor(
                            kmask[:], bc(ksb[:].unsqueeze(2), [128, NW, H, Q]),
                            bc(head_of_row[:].unsqueeze(1).unsqueeze(3), [128, NW, H, Q]),
                            ALU.mult).then_inc(kmask_done, 1)

            @block.tensor
            def _(pe):
                pe.wait_ge(consts, 16 * NCONST)
                pe.wait_ge(ready, 1)
                x2 = xg[:].rearrange("p w q -> p (w q)")
                with pe.Fori(0, PAIRS) as p:
                    with pe.Fori(0, NW) as g:
                        n = p * NW + g
                        pe.wait_ge(x_in, new(n, 16))
                        pe.wait_ge(q_sb, old(n, 2))
                        nc.tensor.matmul(psqk[:, 0:GRP], wq[:], x2, start=True, stop=True)
                        nc.tensor.matmul(psqk[:, GRP:2 * GRP], wk[:], x2, start=True, stop=True).then_inc(qk_done, 1)
                        pe.wait_ge(xr_done, new(n))
                        pe.wait_ge(vbd_done, old(n))
                        for w in range(NW):
                            last = nc.tensor.matmul(psv[:, 128 * w:128 * w + 128],
                                                    xrep[:, w].rearrange("p h q -> p (h q)"), wv[:],
                                                    start=True, stop=True)
                        last.then_inc(v_done, 1)
                        pe.wait_ge(q_sb, new(n, 2))
                        pe.wait_ge(kmask_done, new(n))
                        pe.wait_ge(s1_done, old(n))
                        for w in range(NW):
                            last = nc.tensor.matmul(pss[:, 32 * w:32 * w + 32],
                                                    kmask[:, w].rearrange("p h q -> p (h q)"),
                                                    qbd[:, w].rearrange("p b q -> p (b q)"), start=True, stop=True)
                        last.then_inc(s_done, 1)
                        pe.wait_ge(pt_done, new(n))
                        pe.wait_ge(osb_done, old(n, 2))
                        for w in range(NW):
                            last = nc.tensor.matmul(pso[:, 32 * w:32 * w + 32],
                                                    vbd[:, 2 * w:2 * w + 2].rearrange("p b d -> p (b d)"),
                                                    pt[:, w], start=True, stop=True)
                        last.then_inc(o_done, 1)
                        pe.wait_ge(osb_done, new(n, 2))
                        pe.wait_ge(res_done, old(n))
                        nc.tensor.matmul(psp[:, 0:GRP], wo[:], osb[:].rearrange("p w q -> p (w q)"),
                                         start=True, stop=True).then_inc(p_done, 1)

            @block.scalar
            def _(act):
                nc.scalar.preload_act_table_set("exp_and_others")
                act.wait_ge(consts, 16 * NCONST)
                act.wait_ge(ready, 1)
                q4 = psqk[:, 0:GRP].rearrange("p (w q) -> p w q", q=Q)
                o4 = pso[:, 0:2 * GRP].rearrange("p (w b q) -> p w b q", b=2, q=Q)
                with act.Fori(0, PAIRS) as p:
                    with act.Fori(0, NW) as g:
                        n = p * NW + g
                        act.wait_ge(x_in, new(n, 16))
                        act.wait_ge(v_done, old(n))
                        nc.scalar.activation(xrep[:], bc(xg[:].unsqueeze(2), [128, NW, H, Q]), ACT.Copy).then_inc(xr_done, 1)
                        act.wait_ge(qk_done, new(n))
                        act.wait_ge(kmask_done, old(n))
                        nc.scalar.activation(ksb[:], psqk[:, GRP:2 * GRP].rearrange("p (w q) -> p w q", q=Q),
                                             ACT.Identity, bias=bk[:]).then_inc(k_sb, 1)
                        act.wait_ge(s_done, old(n))
                        for b in range(2):
                            r = slice(64 * b, 64 * b + 64)
                            nc.scalar.activation(qbd[r, :, b, :], q4[r], ACT.Identity, bias=bqs[r, :],
                                                 scale=HE ** -0.5).then_inc(q_sb, 1)
                        act.wait_ge(sub_done, new(n))
                        nc.scalar.activation(st[:], st[:], ACT.Exp).then_inc(exp_done, 1)
                        act.wait_ge(o_done, new(n))
                        act.wait_ge(p_done, old(n))
                        for b in range(2):
                            r = slice(64 * b, 64 * b + 64)
                            nc.scalar.activation(osb[r], o4[r, :, b, :], ACT.Identity, bias=bv[r, :]).then_inc(osb_done, 1)
                        act.wait_ge(p_done, new(n))
                        act.wait_ge(stored, old(n, 16))
                        nc.scalar.activation(res[:], psp[:, 0:GRP].rearrange("p (j a c) -> p a j c", j=NW, a=WS),
                                             ACT.Identity, bias=bo[:]).then_inc(res_done, 1)
                        act.wait_ge(res_done, new(n))
                        act.dma_start(h0[p, :, bass.ds(1 + g * GRP, GRP)],
                                      res[:].rearrange("p a j c -> p (a j c)")).then_inc(stored, 16)
                act.wait_ge(stored, 16 * (PAIRS * NW + 1))

            @block.vector
            def _(dve):
                for w in (wq, wk, wv):
                    nc.vector.memset(w[:], 0.0)
                nc.vector.memset(zero[:], 0.0)
                nc.vector.memset(qbd[:], 0.0)
                nc.vector.memset(wo[:], 0.0).then_inc(memz, 1)
                dve.wait_ge(consts, 16 * NCONST)
                nc.vector.tensor_scalar(bqs[:], bq[:], HE ** -0.5, None, ALU.mult)
                nc.vector.tensor_tensor(bias[:].rearrange("p k w q -> p (k w) q"),
                                        winmask[:].rearrange("p k w q -> p (k w) q"),
                                        bc(pos[:].unsqueeze(1), [128, 2 * NW, Q]), ALU.add).then_inc(ready, 1)
                dve.wait_ge(ready, 1)

                def group(n, last_row):
                    dve.wait_ge(v_done, new(n))
                    dve.wait_ge(o_done, old(n))
                    nc.vector.tensor_tensor(vbd[:], psv[:, 0:NW * 128].rearrange("p (w d) -> p w d", d=D),
                                            bc(head_of_key[:].unsqueeze(1), [128, 2 * NW, D]),
                                            ALU.mult).then_inc(vbd_done, 1)
                    dve.wait_ge(s_done, new(n))
                    dve.wait_ge(pt_done, old(n))
                    nc.vector.tensor_tensor(
                        s1[:], pss[:, 0:2 * GRP].rearrange("p (w b q) -> p w b q", b=2, q=Q),
                        bc(bias[:, last_row].unsqueeze(2), [128, NW, 2, Q]), ALU.add).then_inc(s1_done, 1)
                    dve.wait_ge(s1_done, new(n))
                    nc.vector.transpose(st[:].rearrange("p w q -> p (w q)"),
                                        s1[:].rearrange("p w b q -> p (w b q)")).then_inc(st_done, 1)
                    dve.wait_ge(st_done, new(n))
                    nc.vector.tensor_reduce(mx[:], st[:], AX.X, ALU.max).then_inc(mx_done, 1)
                    dve.wait_ge(mx_done, new(n))
                    nc.vector.tensor_tensor(st[:], st[:], bc(mx[:].unsqueeze(2), [128, 2 * NW, Q]),
                                            ALU.subtract).then_inc(sub_done, 1)
                    dve.wait_ge(exp_done, new(n))
                    nc.vector.tensor_reduce(sm[:], st[:], AX.X, ALU.add).then_inc(sum_done, 1)
                    dve.wait_ge(sum_done, new(n))
                    nc.vector.reciprocal(rs[:], sm[:]).then_inc(rcp_done, 1)
                    dve.wait_ge(rcp_done, new(n))
                    nc.vector.tensor_tensor(s1[:].rearrange("p w b q -> p (w b) q"), st[:],
                                            bc(rs[:].unsqueeze(2), [128, 2 * NW, Q]), ALU.mult).then_inc(nrm_done, 1)
                    dve.wait_ge(nrm_done, new(n))
                    nc.vector.transpose(pt[:].rearrange("p w q -> p (w q)"),
                                        s1[:].rearrange("p w b q -> p (w b q)")).then_inc(pt_done, 1)

                with dve.Fori(0, PAIRS) as p:
                    with dve.Fori(0, NW - 1) as g:
                        group(p * NW + g, 0)
                    group(p * NW + NW - 1, 1)


def spread(nc, eng, pairs, sem):
    for dst, src in pairs:
        eng.dma_start(dst, src).then_inc(sem, 16)
    return 16 * len(pairs)


def gated_memory(nc, a, h0, h1, y2, lg):
    with ExitStack() as ctx:
        m = Mem(nc, ctx, "B")
        P8 = PAIRS
        W = P8 * TILE
        mean, center, same, ident, upto = (m.sb(n, [128, 128]) for n in ("mean", "center", "same", "ident", "upto"))
        wts = {n: m.sb("proj_" + n, [128, 128]) for n in "qkvifo"}
        bias = {n: m.sb("b" + n, [128, 1]) for n in "qkvifo"}
        ibias, scale = m.sb("ibias", [128, 1]), m.sb("scale", [128, 1])
        gate = m.sb("gate", [128, 2 * E])
        gateb = m.sb("gateb", [128, E])
        first = m.sb("first", [128, W])
        eps, eps8 = m.sb("eps", [128, 1]), m.sb("eps8", [128, 1])
        x, xc, sq, r, y = (m.sb(n, [128, W]) for n in ("x", "xc", "sq", "r", "y"))
        q, k, v, li, lf, eo, ef = (m.sb(n, [128, W]) for n in ("q", "k", "v", "li", "lf", "eo", "ef"))
        mm = m.sb("mm", [128, P8, TILE + 1])
        nn = m.sb("nn", [128, P8, TILE + 1])
        ls = m.sb("ls", [128, W])
        fs, iss, pw, bw = (m.sb(n, [128, W]) for n in ("fs", "iss", "pw", "bw"))
        nq, den, wv_ = m.sb("nq", [128, W]), m.sb("den", [128, W]), m.sb("vw", [128, W])
        el = m.sb("el", [128, P8, 3])
        wk = m.sb("wk", [128, 4, 2, TILE])
        sc = m.sb("sc", [128, 2, 4, TILE])
        mem, mems, memt, dm = (m.sb(n, [128, P8, 128]) for n in ("mem", "mems", "memt", "dm"))
        out, o2, hh = m.sb("out", [128, W]), m.sb("o2", [128, W]), m.sb("hh", [128, W])
        yt = m.sb("yt", [128, W])
        lgs = m.sb("lgs", [128, P8, 2, E])
        PA, PB, PC, PD = (m.ps(n, [128, 1024]) for n in ("PA", "PB", "PC", "PD"))

        consts, memz, ready = m.sems("consts memz ready")
        x_in, h_out, y_out, l_out = m.sems("x_in h_out y_out l_out", 16)
        (cen_done, xc_done, sq_done, var_done, ln_done, r_done, y_done, qkvi_done, q_done, k_done, v_done,
         ti_done, fo_done, ef_done, lf_done, eo_done, li_done, lfn_done, m_done, ls_done, d1a_done, d1_done,
         d2_done, d3_done, d4_done, el_done, fs_done, is_done, bw_done, ela_done, u_done, n_done, nq_done,
         w_done, den_done, denc_done, g_done, g2_done, lng_done, pwd_done, pw_done, raw_done, out_done,
         o2_done, ms_done, ln2_done, r2_done, or_done, h_done, cen2_done, xc2_done, sq2_done, var2_done,
         ln3_done, r3_done, y2_done, tr_done, yt_done, lg_done, lgs_done, mems_done, memt_done, memtc_done,
         carry_done) = m.sems(
            "cen_done xc_done sq_done var_done ln_done r_done y_done qkvi_done q_done k_done v_done "
            "ti_done fo_done ef_done lf_done eo_done li_done lfn_done m_done ls_done d1a_done d1_done "
            "d2_done d3_done d4_done el_done fs_done is_done bw_done ela_done u_done n_done nq_done "
            "w_done den_done denc_done g_done g2_done lng_done pwd_done pw_done raw_done out_done "
            "o2_done ms_done ln2_done r2_done or_done h_done cen2_done xc2_done sq2_done var2_done "
            "ln3_done r3_done y2_done tr_done yt_done lg_done lgs_done mems_done memt_done memtc_done "
            "carry_done", 1)
        tp_done, sc_done, wk_done, scm_done, half_done, dm1_done, dm2_done, mem1_done, mem_done = m.sems(
            "tp_done sc_done wk_done scm_done half_done dm1_done dm2_done mem1_done mem_done", 2)
        loads = []
        for b in range(2):
            s = slice(64 * b, 64 * b + 64)
            loads += [(wts["q"][s, s], a["m_Wq"]), (wts["k"][s, s], a["m_Wk"]), (wts["v"][s, s], a["m_Wv"])]
            loads += [(bias[n][s, :], a["m_b" + n].unsqueeze(1)) for n in "qkv"]
            for j, n in enumerate("ifo"):
                loads += [(wts[n][s, s], a["m_Wg"][:, D * j:D * j + D]),
                          (bias[n][s, :], a["m_bg"][D * j:D * j + D].unsqueeze(1))]
            loads += [(ibias[s, :], a["m_input_bias"].unsqueeze(1)), (scale[s, :], a["m_norm_scale"].unsqueeze(1)),
                      (gate[s, E * b:E * b + E], a["e_gate_w"])]
        loads += [(gateb[:], a["e_gate_b"].partition_broadcast(128))]
        loads += [(mean[:], a["c_mean"]), (center[:], a["c_center"]), (same[:], a["c_same"]),
                  (ident[:], a["c_ident"]), (upto[:], a["c_upto"])]
        loads += [(first[:, TILE * p:TILE * p + TILE], a["c_first"]) for p in range(P8)]
        CN = 16 * len(loads)
        m.open()

        def p3(t):
            return t[:].rearrange("p (a t) -> p a t", t=TILE)

        with nc.Block() as block:

            @block.sync
            def _(sp):
                sp.wait_ge(memz, 1)
                spread(nc, sp, loads, consts)
                with sp.Fori(0, CHUNKS) as c:
                    sp.wait_ge(h_done, old(c))
                    sp.dma_start(p3(x), h0[:, :, bass.ds(c * TILE, TILE)].rearrange("a p t -> p a t")).then_inc(x_in, 16)

            @block.gpsimd
            def _(pool):
                pool.wait_ge(consts, CN)

            @block.tensor
            def _(pe):
                pe.wait_ge(consts, CN)
                pe.wait_ge(ready, 1)

                def wide(dst, w, src):
                    for j in range(2):
                        last = nc.tensor.matmul(dst[:, 512 * j:512 * j + 512], w[:], src[:, 512 * j:512 * j + 512],
                                                start=True, stop=True)
                    return last

                with pe.Fori(0, CHUNKS) as c:
                    pe.wait_ge(x_in, new(c, 16))
                    pe.wait_ge(yt_done, old(c))
                    wide(PA, center, x).then_inc(cen_done, 1)
                    pe.wait_ge(mem_done, old(c, 2))
                    pe.wait_ge(lgs_done, old(c))
                    pe.wait_ge(sq_done, new(c))
                    pe.wait_ge(xc2_done, old(c))
                    wide(PB, mean, sq).then_inc(var_done, 1)
                    pe.wait_ge(y_done, new(c))
                    pe.wait_ge(xc_done, new(c))
                    wide(PA, wts["q"], y)
                    pe.wait_ge(ln_done, new(c))
                    wide(PB, wts["k"], y)
                    wide(PC, wts["v"], y)
                    wide(PD, wts["i"], y).then_inc(qkvi_done, 1)
                    pe.wait_ge(q_done, new(c))
                    wide(PA, wts["f"], y)
                    pe.wait_ge(k_done, new(c))
                    wide(PB, wts["o"], y).then_inc(fo_done, 1)
                    pe.wait_ge(nq_done, new(c))
                    pe.wait_ge(v_done, new(c))
                    wide(PC, same, nq).then_inc(den_done, 1)
                    pe.wait_ge(mems_done, new(c))
                    pe.wait_ge(ti_done, new(c))
                    for p in range(P8):
                        last = nc.tensor.transpose(PD[:, 128 * p:128 * p + 128], mems[:, p], ident[:])
                    last.then_inc(memt_done, 1)
                    pe.wait_ge(denc_done, new(c))
                    pe.wait_ge(memtc_done, new(c))
                    pe.wait_ge(w_done, new(c))
                    pe.wait_ge(ef_done, new(c))
                    pe.wait_ge(eo_done, new(c))
                    for half in range(2):
                        for j in range(4):
                            p = 4 * half + j
                            nc.tensor.transpose(PA[:, 256 * j:256 * j + 128], wv_[:, 128 * p:128 * p + 128], ident[:])
                            last = nc.tensor.transpose(PA[:, 256 * j + 128:256 * j + 256], k[:, 128 * p:128 * p + 128], ident[:])
                        last.then_inc(tp_done, 1)
                        for j in range(4):
                            p = 4 * half + j
                            for b in range(2):
                                s = slice(64 * b, 64 * b + 64)
                                last = nc.tensor.matmul(PB[:, 512 * b + 128 * j:512 * b + 128 * j + 128],
                                                        k[s, 128 * p:128 * p + 128], q[s, 128 * p:128 * p + 128],
                                                        start=True, stop=True)
                        last.then_inc(sc_done, 1)
                        pe.wait_ge(wk_done, 2 * c + 3 + half)
                        pe.wait_ge(scm_done, 2 * c + 3 + half)
                        for j in range(4):
                            p = 4 * half + j
                            t = slice(128 * p, 128 * p + 128)
                            nc.tensor.matmul(PC[:, t], memt[:, p], q[:, t], start=True, stop=False, skip_group_check=True)
                            for b in range(2):
                                s = slice(64 * b, 64 * b + 64)
                                last = nc.tensor.matmul(PC[s, t], wk[:, j, 0, s], sc[:, b, j],
                                                        start=False, stop=True, skip_group_check=True)
                        if half:
                            last.then_inc(raw_done, 1)
                        if half:
                            pe.wait_ge(dm1_done, 2 * c + 3)
                        for j in range(4):
                            last = nc.tensor.matmul(PD[:, 128 * j:128 * j + 128], wk[:, j, 0], wk[:, j, 1],
                                                    start=True, stop=True)
                        last.then_inc(half_done, 1)
                    pe.wait_ge(o2_done, new(c))
                    wide(PA, mean, o2).then_inc(ms_done, 1)
                    pe.wait_ge(h_done, new(c))
                    wide(PB, center, hh).then_inc(cen2_done, 1)
                    pe.wait_ge(sq2_done, new(c))
                    pe.wait_ge(out_done, new(c))
                    wide(PC, mean, sq).then_inc(var2_done, 1)
                    pe.wait_ge(y2_done, new(c))
                    pe.wait_ge(ln2_done, new(c))
                    for p in range(P8):
                        last = nc.tensor.transpose(PA[:, 128 * p:128 * p + 128], y[:, 128 * p:128 * p + 128], ident[:])
                    last.then_inc(tr_done, 1)
                    pe.wait_ge(dm1_done, new(c, 2))
                    for p in range(P8):
                        last = nc.tensor.matmul(PD[:, 512 + 16 * p:512 + 16 * p + 16], y[:, 128 * p:128 * p + 128], gate[:],
                                                start=True, stop=True)
                    last.then_inc(lg_done, 1)

            @block.scalar
            def _(act):
                A = nc.scalar.activation
                nc.scalar.preload_act_table_set(LN_EXP)
                act.wait_ge(consts, CN)
                act.wait_ge(ready, 1)
                with act.Fori(0, CHUNKS) as c:
                    act.wait_ge(cen_done, new(c))
                    act.wait_ge(y2_done, old(c))
                    A(xc[:], PA[:], ACT.Copy).then_inc(xc_done, 1)
                    act.wait_ge(var2_done, old(c))
                    A(sq[:], PA[:], ACT.Square).then_inc(sq_done, 1)
                    act.wait_ge(var_done, new(c))
                    A(r[:], PB[:], ACT.Ln, bias=eps[:]).then_inc(ln_done, 1)
                    act.wait_ge(ln_done, new(c))
                    A(r[:], r[:], ACT.Exp, scale=-0.5).then_inc(r_done, 1)
                    act.wait_ge(qkvi_done, new(c))
                    act.wait_ge(half_done, old(c, 2))
                    A(q[:], PA[:], ACT.Identity, bias=bias["q"][:]).then_inc(q_done, 1)
                    A(k[:], PB[:], ACT.Identity, bias=bias["k"][:], scale=D ** -0.5).then_inc(k_done, 1)
                    act.wait_ge(w_done, old(c))
                    A(v[:], PC[:], ACT.Identity, bias=bias["v"][:]).then_inc(v_done, 1)
                    act.wait_ge(d4_done, old(c))
                    A(li[:], PD[:], ACT.Tanh, bias=bias["i"][:], scale=0.1).then_inc(ti_done, 1)
                    nc.scalar.preload_act_table_set(LN_EXP)
                    act.wait_ge(fo_done, new(c))
                    A(ef[:], PA[:], ACT.Exp, bias=bias["f"][:]).then_inc(ef_done, 1)
                    act.wait_ge(g2_done, old(c))
                    A(eo[:], PB[:], ACT.Exp, bias=bias["o"][:], scale=-1.0).then_inc(eo_done, 1)
                    act.wait_ge(ef_done, new(c))
                    act.wait_ge(d1a_done, old(c))
                    A(lf[:], ef[:], ACT.Ln, bias=1.0).then_inc(lf_done, 1)
                    act.wait_ge(d1_done, new(c))
                    act.wait_ge(d2_done, new(c))
                    act.wait_ge(el_done, new(c))
                    A(el[:], el[:], ACT.Exp).then_inc(ela_done, 1)
                    A(fs[:], fs[:], ACT.Exp).then_inc(fs_done, 1)
                    A(iss[:], iss[:], ACT.Exp).then_inc(is_done, 1)
                    act.wait_ge(d4_done, new(c))
                    A(bw[:], bw[:], ACT.Exp).then_inc(bw_done, 1)
                    act.wait_ge(memt_done, new(c))
                    A(memt[:].rearrange("p a j -> p (a j)"), PD[:], ACT.Copy).then_inc(memtc_done, 1)
                    act.wait_ge(den_done, new(c))
                    act.wait_ge(pwd_done, old(c))
                    A(den[:], PC[:], ACT.Abs).then_inc(denc_done, 1)
                    act.wait_ge(g2_done, new(c))
                    A(den[:], den[:], ACT.Ln).then_inc(lng_done, 1)
                    act.wait_ge(pwd_done, new(c))
                    A(pw[:], pw[:], ACT.Exp).then_inc(pw_done, 1)
                    for half in range(2):
                        act.wait_ge(tp_done, 2 * c + 3 + half)
                        act.wait_ge(half_done, 2 * c + 2 + half)
                        A(wk[:].rearrange("p a k t -> p (a k t)"), PA[:], ACT.Copy).then_inc(wk_done, 1)
                    act.wait_ge(out_done, new(c))
                    A(o2[:], out[:], ACT.Square).then_inc(o2_done, 1)
                    act.wait_ge(ms_done, new(c))
                    A(r[:], PA[:], ACT.Ln, bias=eps8[:]).then_inc(ln2_done, 1)
                    act.wait_ge(ln2_done, new(c))
                    A(r[:], r[:], ACT.Exp, scale=-0.5).then_inc(r2_done, 1)
                    act.wait_ge(cen2_done, new(c))
                    A(xc[:], PB[:], ACT.Copy).then_inc(xc2_done, 1)
                    A(sq[:], PB[:], ACT.Square).then_inc(sq2_done, 1)
                    act.wait_ge(h_done, new(c))
                    act.dma_start(h1[:, :, bass.ds(c * TILE, TILE)].rearrange("a p t -> p a t"), p3(hh)).then_inc(h_out, 16)
                    act.wait_ge(var2_done, new(c))
                    A(r[:], PC[:], ACT.Ln, bias=eps[:]).then_inc(ln3_done, 1)
                    act.wait_ge(ln3_done, new(c))
                    A(r[:], r[:], ACT.Exp, scale=-0.5).then_inc(r3_done, 1)
                    act.wait_ge(tr_done, new(c))
                    act.wait_ge(y_out, old(c, 16))
                    A(yt[:], PA[:], ACT.Copy).then_inc(yt_done, 1)
                    act.wait_ge(yt_done, new(c))
                    act.dma_start(y2[c], yt[:]).then_inc(y_out, 16)
                    act.wait_ge(lgs_done, new(c))
                    act.dma_start(lg[c], lgs[:].rearrange("p a b e -> p (a b e)")).then_inc(l_out, 16)
                act.wait_ge(h_out, 16 * (CHUNKS + 1))
                act.wait_ge(y_out, 16 * (CHUNKS + 1))
                act.wait_ge(l_out, 16 * (CHUNKS + 1))

            @block.vector
            def _(dve):
                V = nc.vector
                TT, TS, STT = V.tensor_tensor, V.tensor_scalar, V.scalar_tensor_tensor
                for t in [*wts.values(), gate, mem, dm, mm, nn]:
                    V.memset(t[:], 0.0)
                V.memset(eps[:], EPS)
                V.memset(eps8[:], 1e-8).then_inc(memz, 1)
                dve.wait_ge(consts, CN)
                TT(bias["i"][:], bias["i"][:], ibias[:], ALU.add).then_inc(memz, 1)
                TS(bias["k"][:], bias["k"][:], D ** -0.5, None, ALU.mult)
                TS(bias["o"][:], bias["o"][:], -1.0, None, ALU.mult)
                dve.wait_ge(memz, 2)
                TS(bias["i"][:], bias["i"][:], 0.1, None, ALU.mult).then_inc(ready, 1)
                with dve.Fori(0, CHUNKS) as c:
                    dve.wait_ge(r_done, new(c))
                    dve.wait_ge(xc_done, new(c))
                    TT(y[:], xc[:], r[:], ALU.mult).then_inc(y_done, 1)
                    dve.wait_ge(ti_done, new(c))
                    TS(li[:], li[:], 10.0, None, ALU.mult).then_inc(li_done, 1)
                    dve.wait_ge(eo_done, new(c))
                    TS(eo[:], eo[:], 1.0, None, ALU.add).then_inc(g_done, 1)
                    dve.wait_ge(lf_done, new(c))
                    TS(lf[:], lf[:], -1.0, None, ALU.mult).then_inc(lfn_done, 1)
                    dve.wait_ge(lfn_done, new(c))
                    dve.wait_ge(li_done, new(c))
                    V.tensor_tensor_scan(ls[:], first[:], lf[:], 0.0, ALU.mult, ALU.add).then_inc(ls_done, 1)
                    for p in range(P8):
                        last = V.tensor_tensor_scan(mm[:, p, 1:], lf[:, 128 * p:128 * p + 128], li[:, 128 * p:128 * p + 128],
                                                    mm[:, p, 0:1], ALU.add, ALU.max)
                    last.then_inc(m_done, 1)
                    dve.wait_ge(m_done, new(c))
                    dve.wait_ge(n_done, old(c))
                    TT(p3(fs), p3(lf), mm[:, :, 0:TILE], ALU.add).then_inc(d1a_done, 1)
                    dve.wait_ge(u_done, old(c))
                    TT(p3(iss), p3(li), mm[:, :, 1:], ALU.subtract).then_inc(d2_done, 1)
                    dve.wait_ge(d1a_done, new(c))
                    TT(p3(fs), p3(fs), mm[:, :, 1:], ALU.subtract).then_inc(d1_done, 1)
                    dve.wait_ge(ls_done, new(c))
                    dve.wait_ge(mem_done, old(c, 2))
                    l3 = p3(ls)
                    V.tensor_copy(el[:, :, 0:1], l3[:, :, 63:64])
                    V.tensor_copy(el[:, :, 1:2], l3[:, :, 127:128])
                    TT(el[:, :, 2:3], l3[:, :, 127:128], l3[:, :, 63:64], ALU.subtract).then_inc(el_done, 1)
                    TT(p3(pw), l3, bc(l3[:, :, 63:64], [128, P8, TILE]), ALU.subtract).then_inc(d3_done, 1)
                    dve.wait_ge(d3_done, new(c))
                    TT(bw[:], li[:], pw[:], ALU.subtract).then_inc(d4_done, 1)
                    TT(p3(sq), p3(pw), mm[:, :, 1:], ALU.subtract).then_inc(carry_done, 1)
                    dve.wait_ge(ela_done, new(c))
                    TT(mems[:], mem[:], bc(el[:, :, 0:1], [128, P8, 128]), ALU.mult).then_inc(mems_done, 1)
                    dve.wait_ge(is_done, new(c))
                    dve.wait_ge(k_done, new(c))
                    TT(iss[:], iss[:], k[:], ALU.mult).then_inc(u_done, 1)
                    dve.wait_ge(u_done, new(c))
                    dve.wait_ge(fs_done, new(c))
                    for p in range(P8):
                        last = V.tensor_tensor_scan(nn[:, p, 1:], fs[:, 128 * p:128 * p + 128], iss[:, 128 * p:128 * p + 128],
                                                    nn[:, p, 0:1], ALU.mult, ALU.add)
                    last.then_inc(n_done, 1)
                    dve.wait_ge(n_done, new(c))
                    dve.wait_ge(q_done, new(c))
                    TT(p3(nq), nn[:, :, 1:], p3(q), ALU.mult).then_inc(nq_done, 1)
                    dve.wait_ge(bw_done, new(c))
                    dve.wait_ge(v_done, new(c))
                    TT(wv_[:], v[:], bw[:], ALU.mult).then_inc(w_done, 1)
                    V.tensor_copy(nn[:, :, 0:1], nn[:, :, TILE:])
                    V.tensor_copy(mm[:, :, 0:1], mm[:, :, TILE:])
                    dve.wait_ge(denc_done, new(c))
                    dve.wait_ge(g_done, new(c))
                    STT(den[:], den[:], 1e-6, eo[:], ALU.max, ALU.mult).then_inc(g2_done, 1)
                    dve.wait_ge(lng_done, new(c))
                    dve.wait_ge(carry_done, new(c))
                    TT(pw[:], sq[:], den[:], ALU.subtract).then_inc(pwd_done, 1)
                    for half in range(2):
                        dve.wait_ge(sc_done, 2 * c + 3 + half)
                        dve.wait_ge(half_done, 2 * c + 2 + half)
                        TT(sc[:].rearrange("p a b t -> p (a b) t"), PB[:].rearrange("p (a t) -> p a t", t=TILE),
                           bc(upto[:].unsqueeze(1), [128, 8, TILE]), ALU.mult).then_inc(scm_done, 1)
                        dve.wait_ge(half_done, 2 * c + 3 + half)
                        g = slice(4 * half, 4 * half + 4)
                        for b in range(2):
                            s = slice(64 * b, 64 * b + 64)
                            last = TT(dm[s, g, s], PD[s, 0:512].rearrange("p (a j) -> p a j", j=128)[:, :, s],
                                      bc(el[s, g, 2:3], [64, 4, 64]), ALU.mult)
                        last.then_inc(dm1_done, 1)
                        dve.wait_ge(mems_done, new(c))
                        TT(mem[:, g], mem[:, g], bc(el[:, g, 1:2], [128, 4, 128]), ALU.mult).then_inc(mem1_done, 1)
                        dve.wait_ge(mem1_done, 2 * c + 3 + half)
                        dve.wait_ge(dm1_done, 2 * c + 3 + half)
                        TT(mem[:, g], mem[:, g], dm[:, g], ALU.add).then_inc(mem_done, 1)
                    dve.wait_ge(raw_done, new(c))
                    dve.wait_ge(pw_done, new(c))
                    TT(out[:], PC[:], pw[:], ALU.mult).then_inc(out_done, 1)
                    dve.wait_ge(r2_done, new(c))
                    TT(out[:], out[:], r[:], ALU.mult).then_inc(or_done, 1)
                    dve.wait_ge(or_done, new(c))
                    dve.wait_ge(x_in, new(c, 16))
                    dve.wait_ge(h_out, old(c, 16))
                    STT(hh[:], out[:], scale[:], x[:], ALU.mult, ALU.add).then_inc(h_done, 1)
                    dve.wait_ge(r3_done, new(c))
                    dve.wait_ge(xc2_done, new(c))
                    TT(y[:], xc[:], r[:], ALU.mult).then_inc(y2_done, 1)
                    dve.wait_ge(lg_done, new(c))
                    dve.wait_ge(l_out, old(c, 16))
                    TT(lgs[:].rearrange("p a b e -> p (a b) e"),
                       PD[:, 512:512 + 16 * P8].rearrange("p (a e) -> p a e", e=E),
                       bc(gateb[:].unsqueeze(1), [128, 16, E]), ALU.add).then_inc(lgs_done, 1)


def routing(nc, a, lg, xb, sidx, gidx, keepp):
    with ExitStack() as ctx:
        m = Mem(nc, ctx, "R")
        N = CHUNKS * B
        upto, ones = m.sb("upto", [128, 128]), m.sb("ones", [128, 128])
        real = m.sb("real", [128, N])
        slot = m.sb("slot", [128, E])
        L, X, oh, cum = (m.sb(n, [128, N, E]) for n in ("L", "X", "oh", "cum"))
        tot, inc = m.sb("tot", [128, E, B, CHUNKS]), m.sb("inc", [128, E, B, CHUNKS])
        onesr = m.sb("onesr", [128, N])
        mx, sm, prb, taken, pos, sb_, keep, t1, t2 = (m.sb(n, [128, N]) for n in
                                                      ("mx", "sm", "prb", "taken", "pos", "slotb", "keep", "t1", "t2"))
        si, gi = m.sb("si", [128, N], I32), m.sb("gi", [128, N], I32)
        zero = m.sb("zero", [128, 4096])
        ps = m.ps("ps", [128, 4096])
        loads_in, zdone, zeroed, step, cum_done, cumc_done, tot_done, sub_done, exp_done, stores = m.sems(
            "loads_in zdone zeroed step cum_done cumc_done tot_done sub_done exp_done stores")
        m.open()
        flat = lambda t: t[:].rearrange("p n e -> p (n e)")
        finished = [0]
        cuts = [(j, min(512, N * E - j)) for j in range(0, N * E, 512)]
        with nc.Block() as block:

            @block.sync
            def _(sp):
                sp.dma_start(flat(L).rearrange("p (c k) -> p c k", c=CHUNKS), lg.rearrange("c p k -> p c k")).then_inc(loads_in, 16)
                sp.dma_start(upto[:], a["c_upto"]).then_inc(loads_in, 16)
                sp.dma_start(ones[:], a["c_ones"]).then_inc(loads_in, 16)
                sp.dma_start(real[:], a["c_real"]).then_inc(loads_in, 16)
                sp.dma_start(slot[:], a["c_slot"]).then_inc(loads_in, 16)
                sp.wait_ge(zdone, 1)
                xz = xb.rearrange("(p s) d -> p (s d)", p=128)
                width = E * CAPP * D // 128
                for j in range(0, width, 4096):
                    sp.dma_start(xz[:, j:j + 4096], zero[:]).then_inc(zeroed, 16)
                sp.wait_ge(zeroed, 16 * (width // 4096))

            @block.tensor
            def _(pe):
                pe.wait_ge(loads_in, 80)
                pe.wait_ge(step, 4 + 2 * E)
                for j, n in cuts:
                    last = nc.tensor.matmul(ps[:, j:j + n], upto[:], flat(oh)[:, j:j + n], start=True, stop=True)
                last.then_inc(cum_done, 1)
                pe.wait_ge(cumc_done, 1)
                for j, n in cuts:
                    last = nc.tensor.matmul(ps[:, j:j + n], ones[:], flat(oh)[:, j:j + n], start=True, stop=True)
                last.then_inc(tot_done, 1)

            @block.scalar
            def _(act):
                act.wait_ge(sub_done, 1)
                nc.scalar.activation(flat(X), flat(X), ACT.Exp).then_inc(exp_done, 1)
                act.wait_ge(cum_done, 1)
                nc.scalar.activation(flat(cum), ps[:, 0:N * E], ACT.Copy).then_inc(cumc_done, 1)

            @block.vector
            def _(dve):
                V = nc.vector
                TT, TS, STT = V.tensor_tensor, V.tensor_scalar, V.scalar_tensor_tensor
                done = [0]

                def link(ins):
                    done[0] += 1
                    ins.then_inc(step, 1)
                    dve.wait_ge(step, done[0])

                V.memset(onesr[:], 1.0)
                V.memset(taken[:], 0.0)
                V.memset(zero[:], 0.0).then_inc(zdone, 1)
                dve.wait_ge(loads_in, 80)
                link(V.tensor_reduce(mx[:], L[:], AX.X, ALU.max))
                TT(X[:], L[:], bc(mx[:].unsqueeze(2), [128, N, E]), ALU.subtract).then_inc(sub_done, 1)
                link(TT(L[:], L[:], bc(mx[:].unsqueeze(2), [128, N, E]), ALU.is_equal))
                for e in range(E):
                    link(STT(oh[:, :, e], taken[:], 0.0, L[:, :, e], ALU.is_equal, ALU.mult))
                    link(TT(taken[:], taken[:], L[:, :, e], ALU.add))
                link(TT(oh[:], oh[:], bc(real[:].unsqueeze(2), [128, N, E]), ALU.mult))
                dve.wait_ge(exp_done, 1)
                link(V.tensor_reduce(sm[:], X[:], AX.X, ALU.add))
                link(V.reciprocal(prb[:], sm[:]))
                dve.wait_ge(tot_done, 1)
                link(V.tensor_copy(tot[:], ps[:, 0:N * E].rearrange("p (c b e) -> p e b c", c=CHUNKS, b=B)))
                for e in range(E):
                    last = V.tensor_tensor_scan(inc[:, e].rearrange("p b c -> p (b c)"), onesr[:],
                                                tot[:, e].rearrange("p b c -> p (b c)"), 0.0, ALU.mult, ALU.add)
                link(last)
                link(TT(inc[:].rearrange("p e b c -> p (e b c)"), inc[:].rearrange("p e b c -> p (e b c)"),
                        tot[:].rearrange("p e b c -> p (e b c)"), ALU.subtract))
                link(TT(cum[:].rearrange("p (c b) e -> p c b e", c=CHUNKS), cum[:].rearrange("p (c b) e -> p c b e", c=CHUNKS),
                        inc[:].rearrange("p e b c -> p c b e"), ALU.add))
                link(TT(cum[:], cum[:], oh[:], ALU.mult))
                link(V.tensor_reduce(pos[:], cum[:], AX.X, ALU.add))
                link(TT(cum[:], oh[:], bc(slot[:].unsqueeze(1), [128, N, E]), ALU.mult))
                link(V.tensor_reduce(sb_[:], cum[:], AX.X, ALU.add))
                link(TS(pos[:], pos[:], -1.0, None, ALU.add))
                link(TS(keep[:], pos[:], float(CAP), None, ALU.is_lt))
                link(TT(prb[:], prb[:], keep[:], ALU.mult))
                link(TS(t1[:], pos[:], float(CAP - 1), 0.0, ALU.min, ALU.max))
                link(TT(t1[:], t1[:], sb_[:], ALU.add))
                link(V.tensor_copy(gi[:], t1[:]))
                link(TT(keep[:], keep[:], real[:], ALU.mult))
                link(TS(t2[:], keep[:], -float(2 * E * CAPP), float(2 * E * CAPP), ALU.mult, ALU.add))
                link(TT(t2[:], t2[:], t1[:], ALU.add))
                link(V.tensor_copy(si[:], t2[:]))
                total = done[0]
                assert total > 0
                finished[0] = total

            @block.gpsimd
            def _(pool):
                pool.wait_ge(step, finished[0])
                pool.dma_start(sidx.rearrange("c p b -> p c b"), si[:].rearrange("p (c b) -> p c b", b=B)).then_inc(stores, 16)
                pool.dma_start(gidx.rearrange("c p b -> p c b"), gi[:].rearrange("p (c b) -> p c b", b=B)).then_inc(stores, 16)
                pool.dma_start(keepp.rearrange("c p b -> p c b"), prb[:].rearrange("p (c b) -> p c b", b=B)).then_inc(stores, 16)
                pool.wait_ge(stores, 48)


def dispatch(nc, y2, sidx, xb):
    U = 5
    with ExitStack() as ctx:
        m = Mem(nc, ctx, "S")
        row = [m.sb(f"row{u}", [128, B * D]) for u in range(U)]
        idx = [m.sb(f"idx{u}", [128, B], I32) for u in range(U)]
        row_in = m.sems(" ".join(f"row_in{u}" for u in range(U)))
        sent = m.sems(" ".join(f"sent{u}" for u in range(U)))
        passed, = m.sems("passed")
        m.open()
        with nc.Block() as block:

            @block.sync
            def _(sp):
                def load(c, u):
                    sp.dma_start(row[u][:], y2[c]).then_inc(row_in[u], 16)
                    sp.dma_start(idx[u][:], sidx[c]).then_inc(row_in[u], 16)

                for u in range(U):
                    load(u, u)
                with sp.Fori(1, CHUNKS // U) as r:
                    for u in range(U):
                        sp.wait_ge(sent[u], r * 16 * B)
                        load(r * U + u, u)

            @block.gpsimd
            def _(pool):
                with pool.Fori(0, CHUNKS // U) as r:
                    for u in range(U):
                        pool.wait_ge(row_in[u], r * 32 + 32)
                        stand(pool, passed)
                        for b in range(B):
                            pool.indirect_dma_start(
                                out=xb, out_offset=bass.IndirectOffsetOnAxis(ap=idx[u][:, b:b + 1], axis=0),
                                in_=row[u][:, D * b:D * b + D], in_offset=None,
                                bounds_check=E * CAPP - 1, oob_is_err=False).then_inc(sent[u], 16)
                for u in range(U):
                    pool.wait_ge(sent[u], 16 * B * (CHUNKS // U))


def experts(nc, a, xb, yb):
    with ExitStack() as ctx:
        m = Mem(nc, ctx, "X")
        S4 = BLK // 128
        w1, w2 = m.sb("w1", [D, F]), m.sb("w2", [128, 2, D])
        b1, b2 = m.sb("b1", [128, 2]), m.sb("b2", [128, D])
        ident = m.sb("ident", [128, 128])
        xs = [m.sb(f"xs{u}", [128, S4, D]) for u in range(2)]
        xt = [m.sb(f"xt{u}", [D, BLK]) for u in range(2)]
        hm = [m.sb(f"hm{u}", [128, 2, BLK]) for u in range(2)]
        ys = [m.sb(f"ys{u}", [128, S4, D]) for u in range(2)]
        px = [m.ps(f"px{u}", [128, 512]) for u in range(2)]
        ph = [m.ps(f"ph{u}", [128, 1024]) for u in range(2)]
        py = [m.ps(f"py{u}", [128, 512]) for u in range(2)]
        consts, w_in, passed = m.sems("consts w_in passed")
        w_used, = m.sems("w_used", 1)
        x_in, y_out = m.sems("x_in0 x_in1", 16), m.sems("y_out0 y_out1", 16)
        xt_done, xtc_done, up_done, relu_done, down_done, ys_done = (
            m.sems(f"{n}0 {n}1", 1) for n in ("xt_done", "xtc_done", "up_done", "relu_done", "down_done", "ys_done"))
        m.open()
        R = CAPP // BLK // 2
        xv = xb.rearrange("(k p s) d -> k p (s d)", p=128, s=S4)
        yv = yb.rearrange("(k p s) d -> k p (s d)", p=128, s=S4)
        with nc.Block() as block:

            @block.sync
            def _(sp):
                sp.dma_start(ident[:], a["c_ident"]).then_inc(consts, 16)

                def load(n, u):
                    sp.wait_ge(xt_done[u], old(n))
                    sp.dma_start(xs[u][:].rearrange("p s d -> p (s d)"), xv[n * 2 + u]).then_inc(x_in[u], 16)

                def store(n, u):
                    sp.wait_ge(ys_done[u], new(n))
                    sp.dma_start(yv[n * 2 + u], ys[u][:].rearrange("p s d -> p (s d)")).then_inc(y_out[u], 16)

                for u in range(2):
                    load(0, u)
                with sp.Fori(1, E * R) as n:
                    for u in range(2):
                        load(n, u)
                    for u in range(2):
                        store(n - 1, u)
                for u in range(2):
                    store(E * R - 1, u)
                for u in range(2):
                    sp.wait_ge(y_out[u], 16 * (E * R + 1))

            @block.tensor
            def _(pe):
                pe.wait_ge(consts, 16)
                with pe.Fori(0, E) as e:
                    with pe.Fori(0, R) as r:
                        n = e * R + r
                        pe.wait_ge(w_in, e * 64 + 64)
                        for u in range(2):
                            pe.wait_ge(x_in[u], new(n, 16))
                            pe.wait_ge(xtc_done[u], old(n))
                            stand(pe, passed)
                            for s in range(S4):
                                last = nc.tensor.transpose(px[u][0:D, 128 * s:128 * s + 128], xs[u][:, s], ident[:])
                            last.then_inc(xt_done[u], 1)
                        for u in range(2):
                            pe.wait_ge(xtc_done[u], new(n))
                            pe.wait_ge(relu_done[u], old(n))
                            for f in range(2):
                                last = nc.tensor.matmul(ph[u][:, 512 * f:512 * f + 512], w1[:, 128 * f:128 * f + 128],
                                                        xt[u][:], start=True, stop=True)
                            last.then_inc(up_done[u], 1)
                        for u in range(2):
                            pe.wait_ge(relu_done[u], new(n))
                            pe.wait_ge(ys_done[u], old(n))
                            for s in range(S4):
                                for f in range(2):
                                    last = nc.tensor.matmul(py[u][:, D * s:D * s + D], hm[u][:, f, 128 * s:128 * s + 128],
                                                            w2[:, f], start=f == 0, stop=f == 1)
                            last.then_inc(down_done[u], 1)

            @block.scalar
            def _(act):
                with act.Fori(0, E) as e:
                    act.wait_ge(w_used, e + 1)
                    act.dma_start(w1[:], a["e_w1"][e]).then_inc(w_in, 16)
                    act.dma_start(w2[:], a["e_w2"][e].rearrange("(h f) d -> f h d", h=2)).then_inc(w_in, 16)
                    with nc.allow_non_contiguous_dma(reason="a bias by partition"):
                        act.dma_start(b1[:], a["e_b1"][e].rearrange("(h f) -> f h", h=2)).then_inc(w_in, 16)
                    act.dma_start(b2[:], a["e_b2"][e].partition_broadcast(128)).then_inc(w_in, 16)
                    with act.Fori(0, R) as r:
                        n = e * R + r
                        act.wait_ge(w_in, e * 64 + 64)
                        for u in range(2):
                            act.wait_ge(xt_done[u], new(n))
                            act.wait_ge(up_done[u], old(n))
                            nc.scalar.activation(xt[u][:], px[u][0:D, :], ACT.Copy).then_inc(xtc_done[u], 1)
                        for u in range(2):
                            act.wait_ge(up_done[u], new(n))
                            act.wait_ge(down_done[u], old(n))
                            nc.scalar.activation(hm[u][:, 0], ph[u][:, 0:512], ACT.Relu, bias=b1[:, 0:1])
                            nc.scalar.activation(hm[u][:, 1], ph[u][:, 512:1024], ACT.Relu, bias=b1[:, 1:2]).then_inc(relu_done[u], 1)

            @block.vector
            def _(dve):
                def bias_added(n, u):
                    dve.wait_ge(down_done[u], new(n))
                    dve.wait_ge(y_out[u], old(n, 16))
                    nc.vector.tensor_tensor(ys[u][:], py[u][:, 0:S4 * D].rearrange("p (s d) -> p s d", d=D),
                                            bc(b2[:].unsqueeze(1), [128, S4, D]), ALU.add).then_inc(ys_done[u], 1)

                with dve.Fori(0, E) as e:
                    with dve.Fori(0, R) as r:
                        n = e * R + r
                        dve.wait_ge(w_in, e * 64 + 64)
                        for u in range(2):
                            bias_added(n, u)
                    dve.wait_ge(ys_done[1], (e + 1) * R + 1)
                    dve.sem_inc(w_used, 1)


def combine(nc, a, yb, gidx, keepp, h1, h2):
    U = 5
    with ExitStack() as ctx:
        m = Mem(nc, ctx, "G")
        W = PAIRS * TILE
        ident = m.sb("ident", [128, 128])
        row = [m.sb(f"row{u}", [128, B * D]) for u in range(U)]
        idx = [m.sb(f"idx{u}", [128, B], I32) for u in range(U)]
        prob = [m.sb(f"prob{u}", [128, B]) for u in range(U)]
        hx = [m.sb(f"hx{u}", [128, W]) for u in range(U)]
        ho = [m.sb(f"ho{u}", [128, W]) for u in range(U)]
        ps = [m.ps(f"ps{u}", [128, 1024]) for u in range(4)]
        consts, passed = m.sems("consts passed")
        idx_in, got = (m.sems(" ".join(f"{n}{u}" for u in range(U))) for n in ("idx_in", "got"))
        scaled, turned, h_done = (m.sems(" ".join(f"{n}{u}" for u in range(U)), 1) for n in ("scaled", "turned", "h_done"))
        h_out = m.sems(" ".join(f"h_out{u}" for u in range(U)), 16)
        m.open()
        with nc.Block() as block:

            @block.sync
            def _(sp):
                sp.dma_start(ident[:], a["c_ident"]).then_inc(consts, 16)
                with sp.Fori(0, CHUNKS // U) as r:
                    for u in range(U):
                        c = r * U + u
                        sp.wait_ge(h_done[u], old(r))
                        sp.dma_start(idx[u][:], gidx[c]).then_inc(idx_in[u], 16)
                        sp.dma_start(prob[u][:], keepp[c]).then_inc(idx_in[u], 16)
                        sp.dma_start(hx[u][:].rearrange("p (a t) -> p a t", t=TILE),
                                     h1[:, :, bass.ds(c * TILE, TILE)].rearrange("a p t -> p a t")).then_inc(idx_in[u], 16)

            @block.gpsimd
            def _(pool):
                with pool.Fori(0, CHUNKS // U) as r:
                    for u in range(U):
                        pool.wait_ge(idx_in[u], r * 48 + 48)
                        stand(pool, passed)
                        pool.wait_ge(turned[u], old(r))
                        stand(pool, passed)
                        for b in range(B):
                            pool.indirect_dma_start(
                                out=row[u][:, D * b:D * b + D], out_offset=None, in_=yb,
                                in_offset=bass.IndirectOffsetOnAxis(ap=idx[u][:, b:b + 1], axis=0)).then_inc(got[u], 16)

            @block.vector
            def _(dve):
                with dve.Fori(0, CHUNKS // U) as r:
                    for u in range(U):
                        dve.wait_ge(got[u], r * (16 * B) + 16 * B)
                        r3 = row[u][:].rearrange("p (b d) -> p b d", d=D)
                        nc.vector.tensor_tensor(r3, r3, bc(prob[u][:].unsqueeze(2), [128, B, D]), ALU.mult).then_inc(scaled[u], 1)
                    for u in range(U):
                        dve.wait_ge(turned[u], new(r))
                        dve.wait_ge(idx_in[u], r * 48 + 48)
                        dve.wait_ge(h_out[u], old(r, 16))
                        nc.vector.tensor_tensor(ho[u][:], ps[u % 4][:], hx[u][:], ALU.add).then_inc(h_done[u], 1)

            @block.tensor
            def _(pe):
                pe.wait_ge(consts, 16)
                with pe.Fori(0, CHUNKS // U) as r:
                    for u in range(U):
                        pe.wait_ge(scaled[u], new(r))
                        if u < 4:
                            pe.wait_ge(h_done[u], old(r))
                            if u == 0:
                                pe.wait_ge(h_done[4], old(r))
                        else:
                            pe.wait_ge(h_done[0], new(r))
                        for p in range(PAIRS):
                            last = nc.tensor.transpose(ps[u % 4][:, 128 * p:128 * p + 128],
                                                       row[u][:, 128 * p:128 * p + 128], ident[:])
                        last.then_inc(turned[u], 1)

            @block.scalar
            def _(act):
                with act.Fori(0, CHUNKS // U) as r:
                    for u in range(U):
                        c = r * U + u
                        act.wait_ge(h_done[u], new(r))
                        act.dma_start(h2[:, :, bass.ds(c * TILE, TILE)].rearrange("a p t -> p a t"),
                                      ho[u][:].rearrange("p (a t) -> p a t", t=TILE)).then_inc(h_out[u], 16)
                for u in range(U):
                    act.wait_ge(h_out[u], 16 * (CHUNKS // U + 1))


def image_recurrence(nc, a, h2, h3, y4):
    with ExitStack() as ctx:
        m = Mem(nc, ctx, "D")
        N = 400
        R = TP // N
        mean, center = m.sb("mean", [128, 128]), m.sb("center", [128, 128])
        wih = m.sb("wih", [128, 128])
        whh = m.sb("whh", [128, D])
        b1, b2 = m.sb("b1", [128, 1]), m.sb("b2", [128, 1])
        eps = m.sb("eps", [128, 1])
        x, xc, y, hid = (m.sb(n, [128, PAIRS, N]) for n in ("x", "xc", "y", "hid"))
        r = m.sb("r", [128, PAIRS, N])
        sq = [m.sb(f"sq{u}", [128, N]) for u in range(2)]
        pc = [m.ps(f"pc{u}", [128, 512]) for u in range(2)]
        pv = [m.ps(f"pv{u}", [128, 512]) for u in range(2)]
        px = [m.ps(f"px{u}", [128, 512]) for u in range(2)]
        consts, memz, ready, passed = m.sems("consts memz ready passed")
        x_in, h_out, y_out = m.sems("x_in h_out y_out", 16)
        cen, xcd, sqd, var, lnd = m.sems("cen xcd sqd var lnd", 2 * PAIRS)
        rd, yd = m.sems("rd yd", 2)
        hh_done, = m.sems("hh_done", 2 * PAIRS)
        hid_done, = m.sems("hid_done", 2 * PAIRS)
        x3, = m.sems("x3", 1)
        loads = []
        for b in range(2):
            s = slice(64 * b, 64 * b + 64)
            loads += [(wih[s, s], a["r_W_ih"]), (whh[s, :], a["r_W_hh"]),
                      (b1[s, :], a["r_b_ih"].unsqueeze(1)), (b2[s, :], a["r_b_hh"].unsqueeze(1))]
        loads += [(mean[:], a["c_mean"]), (center[:], a["c_center"])]
        CN = 16 * len(loads)
        m.open()
        with nc.Block() as block:

            @block.sync
            def _(sp):
                sp.wait_ge(memz, 1)
                spread(nc, sp, loads, consts)
                with sp.Fori(0, R) as i:
                    sp.wait_ge(yd, old(i, 2))
                    stand(sp, passed)
                    sp.wait_ge(h_out, old(i, 16))
                    stand(sp, passed)
                    sp.dma_start(x[:], h2[:, :, bass.ds(i * N, N)].rearrange("a p t -> p a t")).then_inc(x_in, 16)
                    sp.wait_ge(x3, new(i))
                    stand(sp, passed)
                    sp.dma_start(h3[:, :, bass.ds(i * N, N)].rearrange("a p t -> p a t"), x[:]).then_inc(h_out, 16)
                    sp.wait_ge(yd, new(i, 2))
                    stand(sp, passed)
                    sp.dma_start(y4[:, :, bass.ds(i * N, N)].rearrange("a p t -> p a t"), y[:]).then_inc(y_out, 16)
                sp.wait_ge(h_out, 16 * (R + 1))
                sp.wait_ge(y_out, 16 * (R + 1))

            @block.tensor
            def _(pe):
                pe.wait_ge(consts, CN)
                pe.wait_ge(ready, 1)

                def norms(i, k):
                    base = i * 2 * PAIRS + PAIRS * k + 2 * PAIRS
                    for p in range(PAIRS):
                        pe.wait_ge(xcd, base + p - 1)
                        pe.wait_ge(sqd, base + p - 1)
                        nc.tensor.matmul(pc[p % 2][:, 0:N], center[:], x[:, p], start=True, stop=True).then_inc(cen, 1)
                        if p:
                            square_mean(base + p - 1, p - 1)
                    square_mean(base + PAIRS - 1, PAIRS - 1)

                def square_mean(at, p):
                    pe.wait_ge(sqd, at + 1)
                    pe.wait_ge(lnd, at - 1)
                    nc.tensor.matmul(pv[p % 2][:, 0:N], mean[:], sq[p % 2][:], start=True, stop=True).then_inc(var, 1)

                with pe.Fori(0, R) as i:
                    pe.wait_ge(x_in, new(i, 16))
                    norms(i, 0)
                    pe.wait_ge(yd, i * 2 + 3)
                    for p in range(PAIRS):
                        at = i * 2 * PAIRS + 2 * PAIRS + 2 * p
                        pe.wait_ge(hid_done, at - 2)
                        first = nc.tensor.matmul(px[p % 2][:, 0:N], wih[:], y[:, p], start=True, stop=False,
                                                 skip_group_check=True)
                        for b in range(2):
                            lo = slice(0, 64)
                            hi = slice(64, 128)
                            src, dst = (hi, lo) if b == 0 else (lo, hi)
                            if p or b:
                                pe.wait_ge(hid_done, at + b)
                                stand(pe, passed)
                                prev = hid[src, p - 1 + b]
                                nc.tensor.matmul(px[p % 2][dst, 0:N], whh[src, :], prev, start=False, stop=True,
                                                 skip_group_check=True).then_inc(hh_done, 1)
                            else:
                                first.then_inc(hh_done, 1)
                    pe.wait_ge(x3, new(i))
                    norms(i, 1)

            @block.scalar
            def _(act):
                A = nc.scalar.activation
                nc.scalar.preload_act_table_set(LN_EXP)
                act.wait_ge(ready, 1)

                def norms(i, k):
                    base = i * 2 * PAIRS + PAIRS * k + 2 * PAIRS

                    def log(p):
                        act.wait_ge(var, base + p + 1)
                        A(r[:, p], pv[p % 2][:, 0:N], ACT.Ln, bias=eps[:]).then_inc(lnd, 1)

                    act.wait_ge(yd, i * 2 + k + 2)
                    for p in range(PAIRS):
                        act.wait_ge(cen, base + p + 1)
                        A(xc[:, p], pc[p % 2][:, 0:N], ACT.Copy).then_inc(xcd, 1)
                        if p >= 2:
                            act.wait_ge(var, base + p - 1)
                        A(sq[p % 2][:], pc[p % 2][:, 0:N], ACT.Square).then_inc(sqd, 1)
                        if p:
                            log(p - 1)
                    log(PAIRS - 1)
                    act.wait_ge(lnd, base + PAIRS)
                    A(r[:], r[:], ACT.Exp, scale=-0.5).then_inc(rd, 1)

                with act.Fori(0, R) as i:
                    norms(i, 0)
                    for p in range(PAIRS):
                        for b in range(2):
                            at = i * 2 * PAIRS + 2 * PAIRS + 2 * p + b
                            s = slice(64 * b, 64 * b + 64)
                            act.wait_ge(hh_done, at + 1)
                            A(hid[s, p], px[p % 2][s, 0:N], ACT.Tanh, bias=b1[s, :]).then_inc(hid_done, 1)
                    nc.scalar.preload_act_table_set(LN_EXP)
                    norms(i, 1)

            @block.vector
            def _(dve):
                V = nc.vector
                V.memset(eps[:], EPS)
                V.memset(wih[:], 0.0).then_inc(memz, 1)
                dve.wait_ge(consts, CN)
                V.tensor_tensor(b1[:], b1[:], b2[:], ALU.add).then_inc(ready, 1)
                with dve.Fori(0, R) as i:
                    dve.wait_ge(rd, i * 2 + 3)
                    dve.wait_ge(y_out, old(i, 16))
                    V.tensor_tensor(y[:], xc[:], r[:], ALU.mult).then_inc(yd, 1)
                    dve.wait_ge(hid_done, new(i, 2 * PAIRS))
                    V.tensor_tensor(x[:], x[:], hid[:], ALU.add).then_inc(x3, 1)
                    dve.wait_ge(rd, i * 2 + 4)
                    V.tensor_tensor(y[:], xc[:], r[:], ALU.mult).then_inc(yd, 1)


def slice_attention(nc, a, h3, y4, out):
    with ExitStack() as ctx:
        m = Mem(nc, ctx, "E")
        C, K1 = CHUNKS, D + 1
        ident = m.sb("ident", [128, 128])
        wxa, wxs = m.sb("wxa", [K1, SH * G]), m.sb("wxs", [K1, SH * G])
        wxt = m.sb("wxt", [D, SH, K1])
        wsl = m.sb("wsl", [D, G])
        unit = m.sb("unit", [1, K1])
        bsl = m.sb("bsl", [1, SH, G])
        temp, rtemp = m.sb("temp", [K1, SH]), m.sb("rtemp", [K1, SH])
        wfx = m.sb("wfx", [K1, SH, K1])
        wqt, wkt, wvt = (m.sb(n, [D, D]) for n in ("wqt", "wkt", "wvt"))
        wout = m.sb("wout", [D, SH, D])
        amat, bmat = m.sb("amat", [D, D]), m.sb("bmat", [D, SH, D])
        res = m.sb("res", [K1, D])
        w = [m.sb(f"w{u}", [128, C, SH * G]) for u in range(2)]
        ya = m.sb("ya", [K1, TP])
        ha = m.sb("ha", [K1, TP])
        ob = m.sb("ob", [128, C, D])
        ytk = [m.sb(f"ytk{u}", [128, K1]) for u in range(3)]
        mx, sm, rs = (([m.sb(f"{n}{u}", [128, SH]) for u in range(3)]) for n in ("mx", "sm", "rs"))
        wts = [m.sb(f"wts{u}", [128, 512]) for u in range(2)]
        zs = m.sb("zs", [K1, SH * G])
        nrm, nrmr = m.sb("nrm", [G, SH]), m.sb("nrmr", [G, SH])
        tok, at = m.sb("tok", [G, SH, D]), m.sb("at", [G, SH, G])
        tokt, ut, att, vb = (m.sb(n, [D, SH, D]) for n in ("tokt", "ut", "att", "vb"))
        amx, asm_, ars = (m.sb(n, [G, SH]) for n in ("amx", "asm", "ars"))
        mo = m.sb("mo", [128, SH // 2, D])
        LG = [m.ps(f"lg{u}", [128, 512]) for u in range(2)]
        Z, YT = m.ps("z", [128, 512]), m.ps("yt", [128, 512])
        WT = [m.ps(f"wt{u}", [128, 512]) for u in range(2)]
        O = [m.ps(f"o{u}", [128, 512]) for u in range(2)]

        consts, fixed, pre, prec, passed = m.sems("consts fixed pre prec passed")
        y_in, h_in = m.sems("y_in h_in", 16)
        o_out, = m.sems("o_out", 32)
        (z_done, zs_done, st_done, nadd_done, nrcp_done, tok_done, tt_done, ttc_done, uv_done, utc_done,
         vbc_done, sc_done, amx_done, asub_done, aexp_done, asum_done, arcp_done, at_done, att_done,
         attc_done, mo_done, moc_done) = m.sems(
            "z_done zs_done st_done nadd_done nrcp_done tok_done tt_done ttc_done uv_done utc_done "
            "vbc_done sc_done amx_done asub_done aexp_done asum_done arcp_done at_done att_done "
            "attc_done mo_done moc_done", 1)
        (lg_done, yt_done, ytc_done, mx_done, sub_done, exp_done, sum_done, rcp_done, w_done, zt_done,
         wt_done, wtc_done, o_done, oc_done) = m.sems(
            "lg_done yt_done ytc_done mx_done sub_done exp_done sum_done rcp_done w_done zt_done "
            "wt_done wtc_done o_done oc_done", 2)

        def tile_done(n, c):
            return n * C + (c + 3)

        loads = [(ident[:], a["c_ident"]), (wxa[0:D, :], a["s_W_x"]), (wxa[D:K1, :], a["s_b_x"].unsqueeze(0)),
                 (wsl[:], a["s_W_slice"]), (unit[:], a["c_ident"][D:D + 1, 0:K1]),
                 (bsl[:], bc(a["s_b_slice"].unsqueeze(0).unsqueeze(0), [1, SH, G])),
                 (temp[:], a["s_temp"].partition_broadcast(K1)),
                 (wfx[0:D, :, 0:D], a["s_W_fx"].rearrange("d (h c) -> d h c", h=SH)),
                 (wfx[D:K1, :, 0:D], a["s_b_fx"].unsqueeze(0).rearrange("o (h c) -> o h c", h=SH)),
                 (wqt[:], a["s_W_q"]), (wkt[:], a["s_W_k"]), (wvt[:], a["s_W_v"]),
                 (wout[:], a["s_W_out"].rearrange("(h e) d -> e h d", h=SH)),
                 (res[0:D, :], a["c_ident"][0:D, 0:D]), (res[D:K1, :], a["s_b_out"].unsqueeze(0))]
        CN = 16 * len(loads)

        steps = [f"s{k}" for k in range(1, 10)]

        def schedule(first, last):
            e1 = [] if last else [("e1", c) for c in range(C)] + [("e1end", 0)]
            if first:
                return e1
            items = []
            for k, s in enumerate(steps):
                items.append((s, 0))
                if k >= 1 and e1:
                    items.append(e1.pop(0))
            e3 = [("e3", c) for c in range(C)] + [("e3end", 0)]
            while e1 or e3:
                if e3:
                    items.append(e3.pop(0))
                if e1:
                    items.append(e1.pop(0))
            return items

        def rounds(eng, parts):
            for it, c in schedule(True, False):
                parts(it, c, 0, 0)
            with eng.Fori(0, B // 2 - 1) as i:
                for u in range(2):
                    n = i * 2 + u
                    for it, c in schedule(False, False):
                        if it.startswith("e1"):
                            parts(it, c, n + 1, 1 - u)
                        else:
                            parts(it, c, n, u)
            for n in (B - 2, B - 1):
                for it, c in schedule(False, n == B - 1):
                    if it.startswith("e1"):
                        parts(it, c, n + 1, 1 - n % 2)
                    else:
                        parts(it, c, n, n % 2)

        m.open()
        with nc.Block() as block:

            @block.sync
            def _(sp):
                spread(nc, sp, loads, consts)
                yv = y4.rearrange("a (b d) t -> (a b) d t", b=2)
                hv = h3.rearrange("a (b d) t -> (a b) d t", b=2)

                sp.dma_start(ya[0:D, :], yv[0]).then_inc(y_in, 16)

                def image(n):
                    sp.wait_ge(o_done, tile_done(n, -1))
                    sp.dma_start(ha[0:D, :], hv[n]).then_inc(h_in, 16)

                def store(n):
                    sp.wait_ge(oc_done, tile_done(n, C - 1))
                    sp.dma_start(out[n, 0:T - TAIL, :].rearrange("(c p) d -> p c d", p=128), ob[:, 0:C - 1]).then_inc(o_out, 16)
                    sp.dma_start(out[n, T - TAIL:T, :], ob[0:TAIL, C - 1]).then_inc(o_out, 16)

                def next_y(n):
                    sp.wait_ge(lg_done, tile_done(n, C - 1))
                    sp.wait_ge(yt_done, tile_done(n, C - 1))
                    sp.dma_start(ya[0:D, :], yv[n + 1]).then_inc(y_in, 16)

                next_y(0)
                image(0)
                with sp.Fori(0, B - 2) as n:
                    next_y(n + 1)
                    stand(sp, passed)
                    store(n)
                    image(n + 1)
                store(B - 2)
                image(B - 1)
                store(B - 1)
                sp.wait_ge(o_out, 32 * (B + 1))

            @block.tensor
            def _(pe):
                mmul, turn = nc.tensor.matmul, nc.tensor.transpose
                pe.wait_ge(consts, CN)
                pe.wait_ge(fixed, 1)
                for h in range(SH):
                    last = turn(WT[h // 4][0:G, K1 * (h % 4):K1 * (h % 4) + K1], wxa[:, G * h:G * h + G], ident[0:K1, 0:K1])
                last.then_inc(pre, 1)
                pe.wait_ge(prec, 1)
                for h in range(SH):
                    mmul(O[0][0:K1, G * h:G * h + G], wxt[:, h], wsl[:], start=True, stop=False, skip_group_check=True)
                    mmul(O[0][0:K1, G * h:G * h + G], unit[:], bsl[:, h], start=False, stop=True, skip_group_check=True)
                mmul(O[1][0:D, 0:D], wqt[:], wkt[:], start=True, stop=True)
                for h in range(SH):
                    last = mmul(LG[0][0:D, D * h:D * h + D], wvt[:], wout[:, h], start=True, stop=True)
                last.then_inc(pre, 1)
                pe.wait_ge(prec, 4)

                def zsum(n, c, u):
                    pe.wait_ge(w_done, tile_done(n, c))
                    pe.wait_ge(ytc_done, tile_done(n, c))
                    k = TAIL if c == C - 1 else 128
                    mmul(Z[0:K1, :], ytk[c % 3][0:k, :], w[u][0:k, c], start=c == 0, stop=c == C - 1).then_inc(zt_done, 1)

                def product(n, c, u):
                    pe.wait_ge(wtc_done, tile_done(n, c))
                    pe.wait_ge(oc_done, tile_done(n, c - 2))
                    pe.wait_ge(h_in, new(n, 16))
                    stand(pe, passed)
                    for k in range(4):
                        mmul(O[c % 2][:, 0:D], wts[c % 2][:, 128 * k:128 * k + 128], mo[:, k], start=k == 0, stop=False)
                    mmul(O[c % 2][:, 0:D], ha[:, 128 * c:128 * c + 128], res[:], start=False, stop=True).then_inc(o_done, 1)

                def parts(it, c, n, u):
                    if it == "e1":
                        if c == 0:
                            pe.wait_ge(y_in, new(n, 16))
                            pe.wait_ge(zs_done, old(n))
                        pe.wait_ge(sub_done, tile_done(n, c - 2))
                        mmul(LG[c % 2][:, :], ya[:, 128 * c:128 * c + 128], wxs[:], start=True, stop=True).then_inc(lg_done, 1)
                        pe.wait_ge(ytc_done, tile_done(n, c - 1))
                        turn(YT[:, 0:K1], ya[:, 128 * c:128 * c + 128], ident[0:K1, 0:K1]).then_inc(yt_done, 1)
                        if c >= 2:
                            zsum(n, c - 2, u)
                    elif it == "e1end":
                        zsum(n, C - 2, u)
                        zsum(n, C - 1, u)
                    elif it == "s2":
                        pe.wait_ge(zs_done, new(n))
                        pe.wait_ge(wtc_done, n * C + 2)
                        stand(pe, passed)
                        for h in range(SH):
                            last = mmul(WT[h // 4][0:G, K1 * (h % 4):K1 * (h % 4) + K1], zs[:, G * h:G * h + G], wfx[:, h],
                                        start=True, stop=True)
                        last.then_inc(st_done, 1)
                    elif it == "s4":
                        pe.wait_ge(tok_done, new(n))
                        pe.wait_ge(oc_done, n * C + 2)
                        stand(pe, passed)
                        for h in range(SH):
                            last = turn(O[0][0:D, D * h:D * h + D], tok[:, h], ident[0:G, 0:G])
                        last.then_inc(tt_done, 1)
                    elif it == "s5":
                        pe.wait_ge(ttc_done, new(n))
                        stand(pe, passed)
                        mmul(WT[0][0:D, :], amat[:], tokt[:].rearrange("p h g -> p (h g)"), start=True, stop=True)
                        for h in range(SH):
                            last = mmul(O[1][0:G, D * h:D * h + D], tokt[:, h], bmat[:, h], start=True, stop=True)
                        last.then_inc(uv_done, 1)
                    elif it == "s6":
                        pe.wait_ge(utc_done, new(n))
                        stand(pe, passed)
                        for h in range(SH):
                            last = mmul(WT[1][0:G, G * h:G * h + G], ut[:, h], tokt[:, h], start=True, stop=True)
                        last.then_inc(sc_done, 1)
                    elif it == "s8":
                        pe.wait_ge(at_done, new(n))
                        stand(pe, passed)
                        for h in range(SH):
                            last = turn(WT[0][0:G, G * h:G * h + G], at[:, h], ident[0:G, 0:G])
                        last.then_inc(att_done, 1)
                    elif it == "s9":
                        pe.wait_ge(attc_done, new(n))
                        pe.wait_ge(vbc_done, new(n))
                        stand(pe, passed)
                        for h in range(SH):
                            last = mmul(O[0][64 * (h % 2):64 * (h % 2) + 64, D * (h // 2):D * (h // 2) + D], att[:, h], vb[:, h],
                                        start=True, stop=True, skip_group_check=True)
                        last.then_inc(mo_done, 1)
                    elif it == "e3":
                        if c == 0:
                            pe.wait_ge(moc_done, new(n))
                        pe.wait_ge(wtc_done, tile_done(n, c - 2))
                        stand(pe, passed)
                        for k in range(4):
                            last = turn(WT[c % 2][:, 128 * k:128 * k + 128], w[u][:, c, 128 * k:128 * k + 128], ident[:])
                        last.then_inc(wt_done, 1)
                        if c:
                            product(n, c - 1, u)
                    elif it == "e3end":
                        product(n, C - 1, u)

                rounds(pe, parts)

            @block.scalar
            def _(act):
                A = nc.scalar.activation
                nc.scalar.preload_act_table_set(TANH)
                act.wait_ge(pre, 1)
                for k in range(2):
                    last = A(wxt[:, 4 * k:4 * k + 4], WT[k][0:D, 0:4 * K1].rearrange("p (h c) -> p h c", c=K1), ACT.Copy)
                last.then_inc(prec, 1)
                act.wait_ge(pre, 2)
                A(amat[:], O[1][0:D, 0:D], ACT.Copy).then_inc(prec, 1)
                A(bmat[:].rearrange("p h d -> p (h d)"), LG[0][0:D, :], ACT.Copy).then_inc(prec, 1)

                def parts(it, c, n, u):
                    if it == "e1":
                        act.wait_ge(yt_done, tile_done(n, c))
                        act.wait_ge(zt_done, tile_done(n, c - 3) if c >= 3 else tile_done(n, -2))
                        A(ytk[c % 3][:], YT[:, 0:K1], ACT.Copy).then_inc(ytc_done, 1)
                        act.wait_ge(sub_done, tile_done(n, c))
                        A(w[u][:, c], w[u][:, c], ACT.Exp).then_inc(exp_done, 1)
                    elif it == "s1":
                        act.wait_ge(zt_done, tile_done(n, C - 1))
                        A(zs[:], Z[0:K1, :], ACT.Copy).then_inc(zs_done, 1)
                    elif it == "s4":
                        act.wait_ge(tt_done, new(n))
                        A(tokt[:].rearrange("p h g -> p (h g)"), O[0][0:D, :], ACT.Copy).then_inc(ttc_done, 1)
                    elif it == "s5":
                        act.wait_ge(uv_done, new(n))
                        A(ut[:].rearrange("p h g -> p (h g)"), WT[0][0:D, :], ACT.Copy).then_inc(utc_done, 1)
                        A(vb[:].rearrange("p h g -> p (h g)"), O[1][0:G, :], ACT.Copy).then_inc(vbc_done, 1)
                    elif it == "s7":
                        act.wait_ge(asub_done, new(n))
                        A(at[:], at[:], ACT.Exp, scale=D ** -0.5).then_inc(aexp_done, 1)
                    elif it == "s8":
                        act.wait_ge(att_done, new(n))
                        A(att[:].rearrange("p h g -> p (h g)"), WT[0][0:G, :], ACT.Copy).then_inc(attc_done, 1)
                    elif it == "s9":
                        act.wait_ge(mo_done, new(n))
                        A(mo[:].rearrange("p k d -> p (k d)"), O[0][:, 0:SH // 2 * D], ACT.Copy).then_inc(moc_done, 1)
                    elif it == "e3":
                        act.wait_ge(wt_done, tile_done(n, c))
                        act.wait_ge(o_done, tile_done(n, c - 2))
                        A(wts[c % 2][:], WT[c % 2][:], ACT.Copy).then_inc(wtc_done, 1)

                rounds(act, parts)

            @block.vector
            def _(dve):
                V = nc.vector
                TT, TS = V.tensor_tensor, V.tensor_scalar
                V.memset(wfx[0:D, :, D:K1], 0.0)
                V.memset(ya[D:K1, :], 1.0)
                V.memset(ha[D:K1, :], 1.0)
                dve.wait_ge(consts, CN)
                V.memset(wfx[D:K1, :, D:K1], 1.0).then_inc(fixed, 1)
                TS(temp[:], temp[:], 0.1, 5.0, ALU.max, ALU.min).then_inc(fixed, 1)
                dve.wait_ge(fixed, 2)
                V.reciprocal(rtemp[:], temp[:]).then_inc(fixed, 1)
                dve.wait_ge(fixed, 3)
                dve.wait_ge(pre, 2)
                TT(wxs[:].rearrange("p (h g) -> p h g", h=SH), O[0][0:K1, :].rearrange("p (h g) -> p h g", h=SH),
                   bc(rtemp[:].unsqueeze(2), [K1, SH, G]), ALU.mult).then_inc(prec, 1)

                def sums(n, c, u):
                    dve.wait_ge(exp_done, tile_done(n, c))
                    V.tensor_reduce(sm[c % 3][:], w[u][:, c].rearrange("p (h g) -> p h g", h=SH), AX.X, ALU.add).then_inc(sum_done, 1)
                    dve.wait_ge(sum_done, tile_done(n, c))
                    dve.wait_ge(w_done, tile_done(n, c - 3) if c >= 3 else tile_done(n, -1))
                    V.reciprocal(rs[c % 3][:], sm[c % 3][:]).then_inc(rcp_done, 1)

                def parts(it, c, n, u):
                    if it == "e1":
                        l3 = LG[c % 2][:].rearrange("p (h g) -> p h g", h=SH)
                        dve.wait_ge(lg_done, tile_done(n, c))
                        V.tensor_reduce(mx[c % 3][:], l3, AX.X, ALU.max).then_inc(mx_done, 1)
                        if c:
                            sums(n, c - 1, u)
                        dve.wait_ge(mx_done, tile_done(n, c))
                        TT(w[u][:, c].rearrange("p (h g) -> p h g", h=SH), l3, bc(mx[c % 3][:].unsqueeze(2), [128, SH, G]),
                           ALU.subtract).then_inc(sub_done, 1)
                    elif it == "e1end":
                        sums(n, C - 1, u)
                    elif it == "s3":
                        dve.wait_ge(st_done, new(n))
                        for k in range(2):
                            last = TS(nrm[:, 4 * k:4 * k + 4].unsqueeze(2),
                                      WT[k][0:G, 0:4 * K1].rearrange("p (h c) -> p h c", c=K1)[:, :, D:K1],
                                      1e-5, None, ALU.add)
                        last.then_inc(nadd_done, 1)
                        dve.wait_ge(nadd_done, new(n))
                        V.reciprocal(nrmr[:], nrm[:]).then_inc(nrcp_done, 1)
                        dve.wait_ge(nrcp_done, new(n))
                        for k in range(2):
                            last = TT(tok[:, 4 * k:4 * k + 4],
                                      WT[k][0:G, 0:4 * K1].rearrange("p (h c) -> p h c", c=K1)[:, :, 0:D],
                                      bc(nrmr[:, 4 * k:4 * k + 4].unsqueeze(2), [G, 4, D]), ALU.mult)
                        last.then_inc(tok_done, 1)
                    elif it == "s7":
                        s3 = WT[1][0:G, :].rearrange("p (h k) -> p h k", h=SH)
                        dve.wait_ge(sc_done, new(n))
                        V.tensor_reduce(amx[:], s3, AX.X, ALU.max).then_inc(amx_done, 1)
                        dve.wait_ge(amx_done, new(n))
                        dve.wait_ge(att_done, old(n))
                        TT(at[:], s3, bc(amx[:].unsqueeze(2), [G, SH, G]), ALU.subtract).then_inc(asub_done, 1)
                        dve.wait_ge(aexp_done, new(n))
                        V.tensor_reduce(asm_[:], at[:], AX.X, ALU.add).then_inc(asum_done, 1)
                        dve.wait_ge(asum_done, new(n))
                        V.reciprocal(ars[:], asm_[:]).then_inc(arcp_done, 1)
                        dve.wait_ge(arcp_done, new(n))
                        TT(at[:], at[:], bc(ars[:].unsqueeze(2), [G, SH, G]), ALU.mult).then_inc(at_done, 1)
                    elif it == "e3" and c:
                        leave(n, c - 1)
                    elif it == "e3end":
                        leave(n, C - 1)

                def leave(n, c):
                    if c == 0:
                        dve.wait_ge(o_out, old(n, 32))
                    dve.wait_ge(o_done, tile_done(n, c))
                    V.tensor_copy(ob[:, c], O[c % 2][:, 0:D]).then_inc(oc_done, 1)

                rounds(dve, parts)

            @block.gpsimd
            def _(pool):
                def parts(it, c, n, u):
                    if it == "e1":
                        w3 = w[u][:, c].rearrange("p (h g) -> p h g", h=SH)
                        pool.wait_ge(rcp_done, tile_done(n, c))
                        nc.gpsimd.tensor_tensor(w3, w3, bc(rs[c % 3][:].unsqueeze(2), [128, SH, G]),
                                                ALU.mult).then_inc(w_done, 1)

                rounds(pool, parts)


def constants():
    import numpy as np
    f = np.float32
    r = np.arange(128)
    c = {}
    c["c_ident"] = np.eye(128, dtype=f)
    same = (r[:, None] // 64 == r[None, :] // 64).astype(f)
    c["c_mean"] = same / f(64)
    c["c_center"] = np.eye(128, dtype=f) - same / f(64)
    c["c_same"] = same
    c["c_upto"] = (r[:, None] <= r[None, :]).astype(f)
    c["c_ones"] = np.ones((128, 128), f)
    hr = (r % 64) // HE
    c["c_head_of_row"] = (hr[:, None] == np.arange(H)[None, :]).astype(f)
    c["c_head_of_key"] = ((r // Q)[:, None] == (np.arange(D) // HE)[None, :]).astype(f)
    far = np.zeros((Q, Q), bool)
    s = WS * (WS // 2)
    far[-s:, :-s] = True
    far[:-s, -s:] = True
    col = far.reshape(WS, WS, WS, WS).transpose(1, 0, 3, 2).reshape(Q, Q)
    w = np.zeros((128, 2, NW, Q), f)
    for k in range(128):
        for last in range(2):
            for j in range(NW):
                m = np.zeros(Q, bool)
                if last:
                    m |= far[:, k % Q]
                if j == NW - 1:
                    m |= col[:, k % Q]
                w[k, last, j] = np.where(m, f(NEG), f(0))
    c["c_winmask"] = w
    c["c_first"] = np.where(r % TILE == 0, f(0), f(1))[None, :].repeat(128, 0).copy()
    real = np.ones((128, B, CHUNKS), f)
    real[TAIL:, :, CHUNKS - 1] = 0
    c["c_real"] = np.ascontiguousarray(real.transpose(0, 2, 1)).reshape(128, CHUNKS * B)
    c["c_slot"] = (np.arange(E) * CAPP).astype(f)[None, :].repeat(128, 0).copy()
    return c


def laid_out(inputs):
    import numpy as np
    g = {k: np.asarray(v) for k, v in inputs.items()}
    a = {}
    x = np.roll(g["x"], (-(WS // 2), -(WS // 2)), axis=(2, 3))
    x = x.reshape(PAIRS, 2 * D, NW, WS, NW, WS).transpose(0, 2, 1, 4, 3, 5)
    a["xw"] = x.reshape(PAIRS * NW, 2 * D, NW, Q)
    w1 = g["L0_tok_w1"].reshape(HE, H, 3, D)
    a["w1"] = w1.transpose(2, 3, 1, 0).reshape(3, D, D)
    a["b1"] = g["L0_tok_b1"].reshape(HE, H, 3).transpose(2, 1, 0).reshape(3, D)
    a["w2"] = g["L0_tok_w2"].T
    a["b2"] = g["L0_tok_b2"]
    a["posr"] = g["L0_tok_pos_emb"][::-1, ::-1]
    a["cls"] = g["cls_tok"].reshape(D)
    for n in ("Wq", "bq", "Wk", "bk", "Wv", "bv", "Wg", "bg", "input_bias", "norm_scale"):
        a["m_" + n] = g["L0_attn_" + n]
    for n in ("gate_w", "gate_b", "w1", "b1", "w2", "b2"):
        a["e_" + n] = g["L0_ffn_" + n]
    a["r_W_ih"] = g["L1_attn_W_ih"].T
    a["r_W_hh"] = g["L1_attn_W_hh"].T
    a["r_b_ih"] = g["L1_attn_b_ih"]
    a["r_b_hh"] = g["L1_attn_b_hh"]
    for n in ("W_fx", "b_fx", "W_x", "b_x", "W_slice", "b_slice", "W_q", "W_k", "W_v", "W_out", "b_out"):
        a["s_" + n] = g["L1_ffn_" + n]
    for n in ("W_q", "W_k", "W_v"):
        a["s_" + n] = a["s_" + n].T
    a["s_temp"] = g["L1_ffn_temperature"].reshape(SH)
    return {k: np.ascontiguousarray(v) for k, v in a.items()}


def program(nc, a, out, upto="Z", dbg=None):
    def scratch(name, shape, dt=F32):
        if dbg is not None and name in dbg:
            return nc.dram_tensor(name, shape, dt, kind="ExternalOutput").ap()
        return nc.dram_tensor(name, shape, dt).ap()

    if upto == "E":
        slice_attention(nc, a, a["h3"], a["y4"], out)
        return
    h0 = scratch("h0", (PAIRS, 128, TP))
    window_attention(nc, a, h0)
    if upto == "A":
        return
    h1 = scratch("h1", (PAIRS, 128, TP))
    y2 = scratch("y2", (CHUNKS, 128, B * D))
    lg = scratch("lg", (CHUNKS, 128, B * E))
    gated_memory(nc, a, h0, h1, y2, lg)
    if upto == "B":
        return
    xb = scratch("xb", (E * CAPP, D))
    yb = scratch("yb", (E * CAPP, D))
    sidx = scratch("sidx", (CHUNKS, 128, B), I32)
    gidx = scratch("gidx", (CHUNKS, 128, B), I32)
    keepp = scratch("keepp", (CHUNKS, 128, B))
    h2 = scratch("h2", (PAIRS, 128, TP))
    routing(nc, a, lg, xb, sidx, gidx, keepp)
    dispatch(nc, y2, sidx, xb)
    experts(nc, a, xb, yb)
    combine(nc, a, yb, gidx, keepp, h1, h2)
    if upto == "C":
        return
    h3 = scratch("h3", (PAIRS, 128, TP))
    y4 = scratch("y4", (PAIRS, 128, TP))
    image_recurrence(nc, a, h2, h3, y4)
    if upto == "D":
        return
    slice_attention(nc, a, h3, y4, out)


def kernel(**inputs):
    import concourse.bacc as bacc
    from concourse.bass_utils import run_bass_kernel_spmd as run

    nc = bacc.Bacc("TRN2", target_bir_lowering=False, num_devices=1)
    arrays = {**laid_out(inputs), **constants()}
    a = {n: nc.dram_tensor("in_" + n, v.shape, mybir.dt.from_np(v.dtype), kind="ExternalInput").ap()
         for n, v in arrays.items()}
    out = nc.dram_tensor("out_0", (B, T, D), F32, kind="ExternalOutput").ap()
    program(nc, a, out)
    r = run(nc, [{"in_" + n: v for n, v in arrays.items()}], core_ids=[0])
    return r.results[0]["out_0"]
```
